# Optimizing a Trainium2 kernel written in Bass

```python
import numpy as np
import jax
import jax.numpy as jnp

def _softmax(x, axis=-1):
    return jax.nn.softmax(x, axis=axis)

def _gelu(x):
    return jax.nn.gelu(x, approximate=True)

def _silu(x):
    return jax.nn.silu(x)

def _sigmoid(x):
    return jax.nn.sigmoid(x)

def _layernorm(x, axis=-1, eps=1e-05):
    m = jnp.mean(x, axis=axis, keepdims=True)
    v = jnp.var(x, axis=axis, keepdims=True)
    return (x - m) / jnp.sqrt(v + eps)

def _scatter_add(tgt, idx, src, axis=0):
    return tgt.at[idx].add(src)

def _segment_sum(src, seg, n):
    return jax.ops.segment_sum(src, seg, n)
kernel_name = 'mk_macaron_d2_jaxref_r4_5e682b'

def setup_inputs(seed: int=0):
    np.random.seed(seed)
    _w = jnp.asarray

    def _L0_attn_setup():
        import jax, jax.numpy as jnp
        import numpy as np
        N_EMBD = 512
        Q_HEAD = 16
        KV_HEAD = 4
        HEAD_DIM = N_EMBD // Q_HEAD
        ROPE_BASE = 10000.0

        def _rope(Y, d_rope, base=ROPE_BASE):
            b, h, t, d = Y.shape
            mid = d_rope // 2
            Y1 = Y[:, :mid]
            Y2 = Y[:, mid:]
            Ym1 = jnp.concatenate([Y1, Y2], axis=1)
            Ym2 = jnp.concatenate([-Y2, Y1], axis=1)
            inv = base ** (-2.0 * jnp.arange(d // 2, dtype=jnp.float32) / d)
            theta = jnp.arange(t, dtype=jnp.float32)[:, None] * inv[None, :]
            cos2 = jnp.concatenate([jnp.cos(theta), jnp.cos(theta)], axis=1)
            sin2 = jnp.concatenate([jnp.sin(theta), jnp.sin(theta)], axis=1)
            return Ym1 * cos2 + Ym2 * sin2

        def _attention(x, Wq, bq, Wk, bk, Wv, bv, Wo, bo):
            b, t, n = x.shape
            hd = n // Q_HEAD
            q = x @ Wq.T + bq
            k = x @ Wk.T + bk
            v = x @ Wv.T + bv
            q = q.reshape(b, t, Q_HEAD, hd).transpose(0, 2, 1, 3)
            k = k.reshape(b, t, KV_HEAD, hd).transpose(0, 2, 1, 3)
            v = v.reshape(b, t, KV_HEAD, hd).transpose(0, 2, 1, 3)
            q = _rope(q, N_EMBD)
            k = _rope(k, N_EMBD)
            rep = Q_HEAD // KV_HEAD
            k = jnp.repeat(k, rep, axis=1)
            v = jnp.repeat(v, rep, axis=1)
            scale = jnp.sqrt(jnp.float32(hd))
            att = jnp.einsum('bhqd,bhkd->bhqk', q, k) / scale
            causal = jnp.tril(jnp.ones((t, t), dtype=bool))
            att = jnp.where(causal[None, None], att, -jnp.inf)
            att = jax.nn.softmax(att, axis=-1)
            y = jnp.einsum('bhqt,bhtd->bhqd', att, v)
            y = y.transpose(0, 2, 1, 3).reshape(b, t, n)
            return y @ Wo.T + bo
        key = jax.random.key(seed)
        ks = jax.random.split(key, 9)
        kv_dim = HEAD_DIM * KV_HEAD
        s = 1.0 / np.sqrt(N_EMBD)
        return {'x': jax.random.normal(ks[0], (4, 256, N_EMBD), jnp.float32), 'Wq': jax.random.normal(ks[1], (N_EMBD, N_EMBD), jnp.float32) * s, 'bq': jax.random.normal(ks[2], (N_EMBD,), jnp.float32) * 0.01, 'Wk': jax.random.normal(ks[3], (kv_dim, N_EMBD), jnp.float32) * s, 'bk': jax.random.normal(ks[4], (kv_dim,), jnp.float32) * 0.01, 'Wv': jax.random.normal(ks[5], (kv_dim, N_EMBD), jnp.float32) * s, 'bv': jax.random.normal(ks[6], (kv_dim,), jnp.float32) * 0.01, 'Wo': jax.random.normal(ks[7], (N_EMBD, N_EMBD), jnp.float32) * s, 'bo': jax.random.normal(ks[8], (N_EMBD,), jnp.float32) * 0.01}
    _L0_attn_in = _L0_attn_setup()

    def _L0_ffn_setup():
        import jax, jax.numpy as jnp
        import numpy as np
        B, S, H, I = (1, 64, 512, 1536)

        def _quantized_matmul(x, w, scale):
            wq = w.astype(jnp.float8_e4m3fn).astype(x.dtype)
            y = jnp.einsum('bsi,io->bso', x, wq)
            return y * scale
        key = jax.random.key(seed)
        ks = jax.random.split(key, 7)
        return {'x': jax.random.normal(ks[0], (B, S, H), dtype=jnp.float32), 'gate_w': jax.random.normal(ks[1], (H, I), dtype=jnp.float32) * 0.02, 'up_w': jax.random.normal(ks[2], (H, I), dtype=jnp.float32) * 0.02, 'down_w': jax.random.normal(ks[3], (I, H), dtype=jnp.float32) * 0.02, 'gate_scale': jax.random.uniform(ks[4], (I,), dtype=jnp.float32, minval=0.5, maxval=1.5), 'up_scale': jax.random.uniform(ks[5], (I,), dtype=jnp.float32, minval=0.5, maxval=1.5), 'down_scale': jax.random.uniform(ks[6], (H,), dtype=jnp.float32, minval=0.5, maxval=1.5)}
    _L0_ffn_in = _L0_ffn_setup()

    def _L1_attn_setup():
        import jax, jax.numpy as jnp
        import numpy as np
        N_HEAD = 16
        key = jax.random.key(seed)
        k1, k2, k3 = jax.random.split(key, 3)
        B, T, C = (2, 512, 512)
        x = jax.random.normal(k1, (B, T, C), dtype=jnp.float32)
        w_attn = jax.random.normal(k2, (C, 3 * C), dtype=jnp.float32) * (1.0 / np.sqrt(C))
        w_proj = jax.random.normal(k3, (C, C), dtype=jnp.float32) * (1.0 / np.sqrt(C))
        return {'x': x, 'w_attn': w_attn, 'w_proj': w_proj}
    _L1_attn_in = _L1_attn_setup()

    def _L1_ffn_setup():
        import jax, jax.numpy as jnp
        import numpy as np
        DIM_IN = 512
        DIM_HIDDEN = 2048
        key = jax.random.key(seed)
        k_x, k_g, k_u, k_d = jax.random.split(key, 4)
        s_in = 1.0 / np.sqrt(DIM_IN)
        s_hid = 1.0 / np.sqrt(DIM_HIDDEN)
        x = jax.random.normal(k_x, (4, 512, DIM_IN), dtype=jnp.float32)
        w_gate = jax.random.uniform(k_g, (DIM_HIDDEN, DIM_IN), jnp.float32, -s_in, s_in)
        w_up = jax.random.uniform(k_u, (DIM_HIDDEN, DIM_IN), jnp.float32, -s_in, s_in)
        w_down = jax.random.uniform(k_d, (DIM_IN, DIM_HIDDEN), jnp.float32, -s_hid, s_hid)
        return {'x': x, 'w_gate': w_gate, 'w_up': w_up, 'w_down': w_down}
    _L1_ffn_in = _L1_ffn_setup()
    _d = {'L0_attn_x': _L0_attn_in['x'], 'L0_attn_Wq': _L0_attn_in['Wq'], 'L0_attn_bq': _L0_attn_in['bq'], 'L0_attn_Wk': _L0_attn_in['Wk'], 'L0_attn_bk': _L0_attn_in['bk'], 'L0_attn_Wv': _L0_attn_in['Wv'], 'L0_attn_bv': _L0_attn_in['bv'], 'L0_attn_Wo': _L0_attn_in['Wo'], 'L0_attn_bo': _L0_attn_in['bo'], 'L0_ffn_gate_w': _L0_ffn_in['gate_w'], 'L0_ffn_up_w': _L0_ffn_in['up_w'], 'L0_ffn_down_w': _L0_ffn_in['down_w'], 'L0_ffn_gate_scale': _L0_ffn_in['gate_scale'], 'L0_ffn_up_scale': _L0_ffn_in['up_scale'], 'L0_ffn_down_scale': _L0_ffn_in['down_scale'], 'L1_attn_w_attn': _L1_attn_in['w_attn'], 'L1_attn_w_proj': _L1_attn_in['w_proj'], 'L1_ffn_w_gate': _L1_ffn_in['w_gate'], 'L1_ffn_w_up': _L1_ffn_in['w_up'], 'L1_ffn_w_down': _L1_ffn_in['w_down']}
    _x0 = _d['L0_attn_x']
    _d['L0_attn_x'] = jax.random.normal(jax.random.fold_in(jax.random.key(seed), 1), (2, 1024, 512), dtype=_x0.dtype)
    del _x0
    return _d

def reference(L0_attn_x, L0_attn_Wq, L0_attn_bq, L0_attn_Wk, L0_attn_bk, L0_attn_Wv, L0_attn_bv, L0_attn_Wo, L0_attn_bo, L0_ffn_gate_w, L0_ffn_up_w, L0_ffn_down_w, L0_ffn_gate_scale, L0_ffn_up_scale, L0_ffn_down_scale, L1_attn_w_attn, L1_attn_w_proj, L1_ffn_w_gate, L1_ffn_w_up, L1_ffn_w_down):

    def _L0_attn_ref(x, Wq, bq, Wk, bk, Wv, bv, Wo, bo):
        import jax, jax.numpy as jnp
        import numpy as np
        N_EMBD = 512
        Q_HEAD = 16
        KV_HEAD = 4
        HEAD_DIM = N_EMBD // Q_HEAD
        ROPE_BASE = 10000.0

        def _rope(Y, d_rope, base=ROPE_BASE):
            b, h, t, d = Y.shape
            mid = d_rope // 2
            Y1 = Y[:, :mid]
            Y2 = Y[:, mid:]
            Ym1 = jnp.concatenate([Y1, Y2], axis=1)
            Ym2 = jnp.concatenate([-Y2, Y1], axis=1)
            inv = base ** (-2.0 * jnp.arange(d // 2, dtype=jnp.float32) / d)
            theta = jnp.arange(t, dtype=jnp.float32)[:, None] * inv[None, :]
            cos2 = jnp.concatenate([jnp.cos(theta), jnp.cos(theta)], axis=1)
            sin2 = jnp.concatenate([jnp.sin(theta), jnp.sin(theta)], axis=1)
            return Ym1 * cos2 + Ym2 * sin2

        def _attention(x, Wq, bq, Wk, bk, Wv, bv, Wo, bo):
            b, t, n = x.shape
            hd = n // Q_HEAD
            q = x @ Wq.T + bq
            k = x @ Wk.T + bk
            v = x @ Wv.T + bv
            q = q.reshape(b, t, Q_HEAD, hd).transpose(0, 2, 1, 3)
            k = k.reshape(b, t, KV_HEAD, hd).transpose(0, 2, 1, 3)
            v = v.reshape(b, t, KV_HEAD, hd).transpose(0, 2, 1, 3)
            q = _rope(q, N_EMBD)
            k = _rope(k, N_EMBD)
            rep = Q_HEAD // KV_HEAD
            k = jnp.repeat(k, rep, axis=1)
            v = jnp.repeat(v, rep, axis=1)
            scale = jnp.sqrt(jnp.float32(hd))
            att = jnp.einsum('bhqd,bhkd->bhqk', q, k) / scale
            causal = jnp.tril(jnp.ones((t, t), dtype=bool))
            att = jnp.where(causal[None, None], att, -jnp.inf)
            att = jax.nn.softmax(att, axis=-1)
            y = jnp.einsum('bhqt,bhtd->bhqd', att, v)
            y = y.transpose(0, 2, 1, 3).reshape(b, t, n)
            return y @ Wo.T + bo
        return _attention(x, Wq, bq, Wk, bk, Wv, bv, Wo, bo)

    def _L0_ffn_ref(x, gate_w, up_w, down_w, gate_scale, up_scale, down_scale):
        import jax, jax.numpy as jnp
        import numpy as np
        B, S, H, I = (1, 64, 512, 1536)

        def _quantized_matmul(x, w, scale):
            wq = w.astype(jnp.float8_e4m3fn).astype(x.dtype)
            y = jnp.einsum('bsi,io->bso', x, wq)
            return y * scale
        gate = jax.nn.silu(_quantized_matmul(x, gate_w, gate_scale))
        up = _quantized_matmul(x, up_w, up_scale)
        fuse = gate * up
        return _quantized_matmul(fuse, down_w, down_scale)

    def _L1_attn_ref(x, w_attn, w_proj):
        import jax, jax.numpy as jnp
        import numpy as np
        N_HEAD = 16
        B, T, C = x.shape
        H = N_HEAD
        D = C // H
        qkv = x @ w_attn
        q, k, v = jnp.split(qkv, 3, axis=-1)
        q = q.reshape(B, T, H, D).transpose(0, 2, 1, 3)
        k = k.reshape(B, T, H, D).transpose(0, 2, 1, 3)
        v = v.reshape(B, T, H, D).transpose(0, 2, 1, 3)
        scale = 1.0 / np.sqrt(D).astype(np.float32)
        att = jnp.einsum('bhqd,bhkd->bhqk', q, k) * scale
        causal = jnp.tril(jnp.ones((T, T), dtype=bool))
        att = jnp.where(causal[None, None, :, :], att, jnp.float32(-jnp.inf))
        att = jax.nn.softmax(att, axis=-1)
        y = jnp.einsum('bhqk,bhkd->bhqd', att, v)
        y = y.transpose(0, 2, 1, 3).reshape(B, T, C)
        return y @ w_proj

    def _L1_ffn_ref(x, w_gate, w_up, w_down):
        import jax, jax.numpy as jnp
        import numpy as np
        DIM_IN = 512
        DIM_HIDDEN = 2048
        gate = jnp.einsum('bsd,hd->bsh', x, w_gate)
        up = jnp.einsum('bsd,hd->bsh', x, w_up)
        gated = jax.nn.silu(gate) * up
        return jnp.einsum('bsh,dh->bsd', gated, w_down)
    x = L0_attn_x
    x = x + 0.5 * _L0_ffn_ref(_layernorm(x, axis=-1), L0_ffn_gate_w, L0_ffn_up_w, L0_ffn_down_w, L0_ffn_gate_scale, L0_ffn_up_scale, L0_ffn_down_scale)
    x = x + _L0_attn_ref(_layernorm(x, axis=-1), L0_attn_Wq, L0_attn_bq, L0_attn_Wk, L0_attn_bk, L0_attn_Wv, L0_attn_bv, L0_attn_Wo, L0_attn_bo)
    x = x + 0.5 * _L0_ffn_ref(_layernorm(x, axis=-1), L0_ffn_gate_w, L0_ffn_up_w, L0_ffn_down_w, L0_ffn_gate_scale, L0_ffn_up_scale, L0_ffn_down_scale)
    x = x + 0.5 * _L1_ffn_ref(_layernorm(x, axis=-1), L1_ffn_w_gate, L1_ffn_w_up, L1_ffn_w_down)
    x = x + _L1_attn_ref(_layernorm(x, axis=-1), L1_attn_w_attn, L1_attn_w_proj)
    x = x + 0.5 * _L1_ffn_ref(_layernorm(x, axis=-1), L1_ffn_w_gate, L1_ffn_w_up, L1_ffn_w_down)
    return x

_drawn_inputs = setup_inputs


def setup_inputs(seed=0):
    import zlib

    import numpy as np

    out = dict(_drawn_inputs(seed))
    spreads = {}
    factors = {'L0_attn_bq': 31.379, 'L0_attn_bk': 36.531, 'L0_attn_bv': 3.65, 'L0_attn_bo': 4.43}
    for name, (base, spread) in spreads.items():
        noise = np.random.default_rng([zlib.crc32(name.encode()), seed]).standard_normal(out[name].shape)
        drawn = base * np.exp(spread * noise) if base else spread * noise
        out[name] = jnp.asarray(drawn.astype(out[name].dtype))
    for name, factor in factors.items():
        out[name] = (out[name] * factor).astype(out[name].dtype)
    return out
```

```python
from contextlib import ExitStack

import numpy as np

import concourse.bass as bass
from concourse import mybir

F32 = mybir.dt.float32
F32R = mybir.dt.float32r
F16 = mybir.dt.float16
BF16 = mybir.dt.bfloat16
FP8 = mybir.dt.float8e4
ALU = mybir.AluOpType
ACT = mybir.ActivationFunctionType
AX = mybir.AxisListType

P = 128
BATCH, SEQ, D = 2, 1024, 512
TOK = BATCH * SEQ
NT = TOK // P
ST = SEQ // P
KT = D // P
CH = 512
NC = TOK // CH
CT = CH // P
HEADS, HD = 16, 32
HPG = P // HD
KV0 = 4
VW = 98
EPS = 1e-5
MASKED = -1e30
FP8_TRN_MAX = 240.0
FP8_FN_MAX = 448.0
NAN_SCALE = 3.4e38 / 464.0
P_SCALE_LN = float(np.log(1024.0))


class Lane:

    def __init__(self, name):
        self.name, self.ops, self.seen, self.last = name, [], {}, None

    def need(self, *tokens):
        for t in tokens:
            if isinstance(t, list):
                self.need(*t)
            elif t is not None and self.seen.get(t[0].name, 0) < t[1]:
                self.seen[t[0].name] = t[1]
                self.ops.append((None, t[0].handle, t[1]))

    def do(self, emit, *tokens, mark=None):
        self.need(*tokens)
        token = mark.up(1) if mark else None
        self.ops.append((emit, mark.handle if mark else None, 1))
        self.last = token
        return token

    def dma(self, out, in_, *tokens, mark):
        self.need(*tokens)
        token = mark.up(16)
        self.ops.append((lambda e, out=out, in_=in_: e.dma_start(out, in_), mark.handle, 16))
        return token

    def play(self, engine):
        for emit, sem, value in self.ops:
            if emit is None:
                engine.wait_ge(sem, value)
            else:
                ins = emit(engine)
                if sem is not None:
                    ins.then_inc(sem, value)


class Sem:
    def __init__(self, ctx, nc, name):
        self.name, self.handle, self.count = name, ctx.enter_context(nc.semaphore(name)), 0

    def up(self, by):
        self.count += by
        return self, self.count


class Ring:

    def __init__(self, views, free=()):
        self.views, self.free, self.at = views, [list(free) for _ in views], 0

    def take(self):
        i = self.at % len(self.views)
        self.at += 1
        return i, self.views[i], self.free[i]


class Banks:

    def __init__(self, view):
        self.view, self.n = view, view.shape[1]
        self.free, self.at = [[] for _ in range(self.n)], 0

    def take(self, width=1):
        if self.at + width > self.n:
            self.at = 0
        i = self.at
        self.at = (i + width) % self.n
        free = [t for f in self.free[i:i + width] for t in f]
        for k in range(i, i + width):
            self.free[k] = free
        return self.view[:, i:i + width, :], free


def build(nc, a, out):
    with ExitStack() as ctx:
        pe, act, dve, pool, sp = (Lane(n) for n in ("pe", "act", "dve", "pool", "sp"))
        sems = {}

        def S(name):
            if name not in sems:
                sems[name] = Sem(ctx, nc, name)
            return sems[name]

        def sbuf(scope, name, shape, dt=F32):
            return scope.enter_context(nc.sbuf_tensor(name, shape, dt))

        x = sbuf(ctx, "x", [P, NT, D])
        hA = [sbuf(ctx, f"hA_{p}", [P, KT, SEQ], F32R) for p in ("hi", "lo")]
        ident = sbuf(ctx, "ident", [P, P])
        ident_b = sbuf(ctx, "ident_b", [P, P], BF16)
        mask_q = sbuf(ctx, "mask_q", [P, P], BF16)
        mask_k = sbuf(ctx, "mask_k", [P, P], BF16)
        stats = sbuf(ctx, "stats", [P, CT, 6])
        meanvar = sbuf(ctx, "meanvar", [P, NT, 2])
        rstd = sbuf(ctx, "rstd", [P, NT])
        minus_half = sbuf(ctx, "minus_half", [P, CT])
        p_scale = sbuf(ctx, "p_scale", [P, 1])
        tmp = [sbuf(ctx, f"tmp{i}", [P, D]) for i in range(2)]

        psum = ctx.enter_context(nc.psum_tensor("psum", [P, 6, 512], F32))
        acc = ctx.enter_context(nc.psum_tensor("acc", [P, 2, 512], F32))
        slots = Banks(psum[:, :, :])
        banks = Ring([acc[:, 0, :], acc[:, 1, :]])
        tmps = Ring(tmp)

        c0 = pool.do(lambda e: e.memset(ident[:], 0.0), mark=S("const"))
        c1 = pool.do(lambda e: e.memset(ident_b[:], 0.0), mark=S("const"))
        c2 = pool.do(lambda e: e.memset(mask_q[:], 0.0), mark=S("const"))
        c3 = pool.do(lambda e: e.memset(mask_k[:], 0.0), mark=S("const"))
        pool.do(lambda e: e.memset(minus_half[:], -0.5), mark=S("const"))
        pool.do(lambda e: e.memset(p_scale[:], P_SCALE_LN), mark=S("const"))
        for t in (ident, ident_b):
            pool.do(lambda e, t=t: e.affine_select(
                out=t[:], in_=t[:], compare_op=ALU.not_equal, fill=1.0, base=0,
                pattern=[[-1, P]], channel_multiplier=1), c0, c1, c2, c3, mark=S("const"))
        pool.do(lambda e: e.affine_select(
            out=mask_q[:], in_=mask_q[:], compare_op=ALU.is_ge, fill=MASKED, base=0,
            pattern=[[-1, P]], channel_multiplier=1), mark=S("const"))
        consts = pool.do(lambda e: e.affine_select(
            out=mask_k[:], in_=mask_k[:], compare_op=ALU.is_ge, fill=MASKED, base=0,
            pattern=[[1, P]], channel_multiplier=-1), mark=S("const"))

        x_rows = a["x"].rearrange("(t p) d -> t p d", p=P)
        x_ready = [sp.dma(x[:, t, :], x_rows[t], mark=S(f"x_in{t // CT}")) for t in range(NT)]
        x_ready = [x_ready[t // CT * CT + CT - 1] for t in range(NT)]
        x_read = [None] * NT

        def mm(out_, lhsT, rhs, start, stop, skip=False):
            return lambda e: e.matmul(out_, lhsT, rhs, start=start, stop=stop,
                                      skip_group_check=skip)

        def passes(out_, terms, *tokens, mark=None):
            pe.need(*tokens)
            for n, (w, m) in enumerate(terms):
                last = n == len(terms) - 1
                t = pe.do(mm(out_, w, m, n == 0, last), mark=mark if last else None)
            return t

        HI, LO = 0, 1
        THREE = ((HI, HI), (HI, LO), (LO, HI))

        def norm_stats(c):
            for i in range(CT):
                t = c * CT + i
                st = dve.do(lambda e, i=i, t=t: e.bn_stats(stats[:, i, :], x[:, t, :]),
                            x_ready[t], S_last.get("stats"), mark=S("ln_stats"))
            for i in range(CT):
                t = c * CT + i
                ag = dve.do(lambda e, i=i, t=t: e.bn_aggr(meanvar[:, t, :], stats[:, i, :]),
                            st, mark=S("ln_stats"))
            S_last["stats"] = ag
            tiles = slice(c * CT, (c + 1) * CT)
            ve = pool.do(lambda e: e.tensor_scalar(rstd[:, tiles], meanvar[:, tiles, 1], EPS, None,
                                                   ALU.add), ag, S_last.get("rstd"), mark=S("ln_rstd"))
            rs = pool.do(lambda e: e.tensor_tensor(rstd[:, tiles], rstd[:, tiles], minus_half[:],
                                                   ALU.pow), ve, consts, mark=S("ln_rstd"))
            return rs

        S_last = {}

        def norm_tile(t, rs, h, at, h_free):
            _, buf, free = tmps.take()
            hn = dve.do(lambda e: e.tensor_scalar(buf[:], x[:, t, :], meanvar[:, t, 0:1],
                                                  rstd[:, t:t + 1], ALU.subtract, ALU.mult),
                        rs, free, mark=S("ln_out"))
            S_last["rstd"] = hn
            ps, ps_free = slots.take()
            pe.need(hn, ps_free, consts)
            for k in range(KT):
                tp = pe.do(lambda e, k=k: e.transpose(ps[:, 0, k * P:(k + 1) * P],
                                                      buf[:, k * P:(k + 1) * P], ident[:]),
                           mark=S("ln_tp") if k == KT - 1 else None)
            free[:] = [tp]
            src = ps[:, 0, :].rearrange("p (k q) -> p k q", k=KT)
            return split_psum(src, [q[:, :, at:at + P] for q in h], tp, h_free, ps_free, "ln")

        def split_psum(src, dst, ready, dst_free, src_free, tag, scale=None):
            hi = act.do(lambda e: e.activation(dst[HI], src, ACT.Copy,
                                               scale=1.0 if scale is None else scale),
                        ready, dst_free, mark=S(f"{tag}_hi"))
            hi32 = dst[HI].bitcast(F32)
            if scale is None:
                lo = dve.do(lambda e: e.tensor_tensor(dst[LO], src, hi32, ALU.subtract),
                            hi, dst_free, mark=S(f"{tag}_lo"))
            else:
                lo = dve.do(lambda e: e.scalar_tensor_tensor(dst[LO], src, scale, hi32, ALU.mult,
                                                             ALU.subtract),
                            hi, dst_free, mark=S(f"{tag}_lo"))
            src_free[:] = [lo]
            return [hi, lo]

        def ends():
            return [l.last for l in (pe, act, dve, pool) if l.last is not None]

        hA_free = [[] for _ in range(2)]

        def ffn(tag, gate_d, up_d, down_d, hidden, gw, scales, quantised):
            with ExitStack() as sc:
                begin = ends()
                groups, MT = hidden // gw, gw // P
                parts = 1 if quantised else 2
                hB = [sbuf(sc, f"{tag}hB{p}", [P, KT, SEQ], F32R) for p in range(2)]
                h = [[q[:, :, c % 2 * CH:(c % 2 + 1) * CH] for q in (hA, hB)[c // 2]]
                     for c in range(NC)]
                h_free = [hA_free[0], hA_free[1], list(begin), list(begin)]
                wn = KT * gw
                w = [[[sbuf(sc, f"{tag}w{n}{b}{p}", [P, wn], F32R) for p in range(parts)]
                      for n in range(3)] for b in range(2)]
                w_free = [list(begin), list(begin)]
                raw = Ring([sbuf(sc, f"{tag}raw{i}", [P, wn]) for i in range(2)], begin)
                act_ = [[sbuf(sc, f"{tag}a{b}{p}", [P, MT, CH], F32R) for p in range(2)]
                        for b in range(2)]
                a_free = [list(begin), list(begin)]
                silu = Ring([sbuf(sc, f"{tag}silu{i}", [P, CH]) for i in range(2)], begin)
                prod = Ring([sbuf(sc, f"{tag}prod{i}", [P, CH]) for i in range(2)], begin)
                if quantised:
                    q8 = [sbuf(sc, f"{tag}q8{i}", [P, wn], FP8) for i in range(2)]
                    qb = [sbuf(sc, f"{tag}qb{i}", [P, wn], BF16) for i in range(3)]
                    qz = sbuf(sc, f"{tag}qz", [P, wn])
                    q_free = list(begin)
                    gs = sbuf(sc, f"{tag}gs", [P, hidden // P])
                    us = sbuf(sc, f"{tag}us", [P, hidden // P])
                    ds = sbuf(sc, f"{tag}ds", [P, D])
                    dso = [sbuf(sc, f"{tag}dso{i}", [P, D]) for i in range(2)]
                    dso = Ring(dso, begin)
                    sp.dma(gs[:], scales[0], begin, mark=S("scales"))
                    sp.dma(us[:], scales[1], mark=S("scales"))
                    sc_in = sp.dma(ds[:], scales[2], mark=S("scales"))

                def load_weights(g):
                    b = g % 2
                    tokens = []
                    for n, src in enumerate((gate_d, up_d, down_d)):
                        i, rb, r_free = raw.take()
                        landed = sp.dma(rb[:], src[g], r_free, mark=S(f"raw{i}"))
                        dst = [q[:] for q in w[b][n]]
                        if quantised:
                            tokens += round_fp8(rb[:], dst[0], landed, w_free[b], r_free)
                        else:
                            hi = pool.do(lambda e, d=dst, r=rb: e.tensor_copy(d[HI], r[:]),
                                         landed, w_free[b], mark=S("w_hi"))
                            lo = pool.do(lambda e, d=dst, r=rb: e.tensor_tensor(
                                d[LO], r[:], d[HI].bitcast(F32), ALU.subtract), hi, mark=S("w_lo"))
                            r_free[:] = [lo]
                            tokens += [hi, lo]
                    return tokens

                def round_fp8(src, dst, landed, dst_free, r_free):
                    one = act.do(lambda e: e.activation(q8[0][:], src, ACT.Copy, saturate=False),
                                 landed, q_free, mark=S("q8"))
                    half = act.do(lambda e: e.activation(q8[1][:], src, ACT.Copy, scale=0.5,
                                                         saturate=False), mark=S("q8"))
                    r_free[:] = [half]
                    m = FP8_TRN_MAX
                    low = dve.do(lambda e: e.tensor_scalar(qb[0][:], q8[0][:], m, -m, ALU.min,
                                                           ALU.max), one, q_free, mark=S("q_dve"))
                    clp = dve.do(lambda e: e.tensor_scalar(qb[1][:], q8[1][:], m / 2, -m / 2,
                                                           ALU.min, ALU.max), half, mark=S("q_dve"))
                    over = pool.do(lambda e: e.tensor_tensor(qb[2][:], q8[1][:], qb[1][:],
                                                             ALU.subtract), clp, q_free,
                                   mark=S("q_pool"))
                    q = dve.do(lambda e: e.scalar_tensor_tensor(qb[0][:], qb[2][:], 2.0, qb[0][:],
                                                                ALU.mult, ALU.add), low, over,
                               mark=S("q_dve"))
                    z = dve.do(lambda e: e.tensor_scalar(qz[:], qb[0][:], NAN_SCALE, 0.0, ALU.mult,
                                                         ALU.mult), q, q_free, mark=S("q_dve"))
                    res = pool.do(lambda e: e.tensor_tensor(dst, qb[0][:], qz[:], ALU.add), z,
                                  dst_free, mark=S("q_pool"))
                    q_free[:] = [res]
                    return [res]

                def gate_up(g, c, n, w_in, h_in):
                    b, wb = n % 2, w[g % 2]
                    views = [[q[:].rearrange("p (k m) -> p k m", k=KT) for q in wb[i]]
                             for i in range(2)]
                    pairs = ((HI, HI), (HI, LO)) if quantised else THREE
                    done, late = [], None
                    for m in range(MT):
                        mt = g * MT + m
                        ps, ps_free = slots.take(2)
                        toks = []
                        for i in range(2):
                            terms = [(views[i][wp][:, k, m * P:(m + 1) * P], h[c][hp][:, k, :])
                                     for k in range(KT) for wp, hp in pairs]
                            toks.append(passes(ps[:, i, :], terms, ps_free, w_in[g % 2], h_in,
                                               mark=S("gate_up")))
                        _, s, s_free = silu.take()
                        _, pr, p_free = prod.take()
                        if quantised:
                            sl = act.do(lambda e, s=s, ps=ps, mt=mt: e.activation(
                                s[:], ps[:, 0, :], ACT.Silu, scale=gs[:, mt:mt + 1]),
                                toks[0], s_free, sc_in, mark=S("silu"))
                            pt = dve.do(lambda e, s=s, ps=ps, pr=pr, mt=mt: e.scalar_tensor_tensor(
                                pr[:], ps[:, 1, :], us[:, mt:mt + 1], s[:], ALU.mult, ALU.mult),
                                toks[1], sl, p_free, sc_in, mark=S("prod"))
                        else:
                            sl = act.do(lambda e, s=s, ps=ps: e.activation(
                                s[:], ps[:, 0, :], ACT.Silu), toks[0], s_free, mark=S("silu"))
                            pt = dve.do(lambda e, s=s, ps=ps, pr=pr: e.tensor_tensor(
                                pr[:], ps[:, 1, :], s[:], ALU.mult), toks[1], sl, p_free,
                                mark=S("prod"))
                        s_free[:] = [pt]
                        ps_free[:] = [sl, pt]
                        hi = act.do(lambda e, pr=pr, m=m: e.activation(
                            act_[b][HI][:, m, :], pr[:], ACT.Copy), pt, a_free[b], mark=S("a_hi"))
                        if late:
                            done.append(late())

                        def late(pr=pr, m=m, hi=hi, p_free=p_free):
                            lo = dve.do(lambda e: e.tensor_tensor(
                                act_[b][LO][:, m, :], pr[:], act_[b][HI][:, m, :].bitcast(F32),
                                ALU.subtract), hi, a_free[b], mark=S("a_lo"))
                            p_free[:] = [lo]
                            return lo
                    done.append(late())
                    h_free[c][:] = [toks[1]]
                    return [done[-1], hi]

                def down(g, c, n, a_in, w_in):
                    b = n % 2
                    wd = [q[:].rearrange("p (m d) -> p m d", m=MT) for q in w[g % 2][2]]
                    pairs = ((HI, HI), (LO, HI)) if quantised else THREE
                    for i in range(CT):
                        t = c * CT + i
                        _, bank, free = banks.take()
                        terms = [(act_[b][ap][:, m, i * P:(i + 1) * P], wd[wp][:, m, :])
                                 for m in range(MT) for ap, wp in pairs]
                        y = passes(bank, terms, free, a_in, w_in[g % 2], mark=S("down"))
                        if quantised:
                            _, o, o_free = dso.take()
                            ev = dve.do(lambda e, o=o, bank=bank: e.scalar_tensor_tensor(
                                o[:], bank, 0.5, ds[:], ALU.mult, ALU.mult), y, o_free, sc_in,
                                mark=S("x_add"))
                            x_ready[t] = pool.do(lambda e, t=t, o=o: e.tensor_tensor(
                                x[:, t, :], x[:, t, :], o[:], ALU.add), ev, x_ready[t], S_last.get("rstd"),
                                mark=S("x_pool"))
                            o_free[:] = [x_ready[t]]
                            free[:] = [ev]
                        else:
                            x_ready[t] = dve.do(lambda e, t=t, bank=bank: e.scalar_tensor_tensor(
                                x[:, t, :], bank, 0.5, x[:, t, :], ALU.mult, ALU.add), y,
                                x_ready[t], mark=S("x_add"))
                            free[:] = [x_ready[t]]
                    a_free[b][:] = [y]
                    w_free[g % 2][:] = [y]

                w_in = [None, None]
                w_in[0] = load_weights(0)
                h_in = [None] * NC

                def norm(c):
                    rs = norm_stats(c)
                    h_in[c] = []
                    for i in range(CT):
                        h_in[c] += norm_tile(c * CT + i, rs, h[c], i * P, h_free[c])

                norm(0)
                pending = None
                n = 0
                for g in range(groups):
                    for c in range(NC):
                        if c == 1 and g + 1 < groups:
                            w_in[(g + 1) % 2] = load_weights(g + 1)
                        a_in = gate_up(g, c, n, w_in, h_in[c])
                        if g == 0 and c + 1 < NC:
                            norm(c + 1)
                        if pending:
                            down(*pending, w_in)
                        pending = (g, c, n, a_in)
                        n += 1
                down(*pending, w_in)

        def attention(tag, wd, kv_heads, scale, bias=None):
            grouped = kv_heads < HEADS
            with ExitStack() as sc:
                begin = ends()
                wbuf = sbuf(sc, f"{tag}w", [P, 2, 4, D], F32R)
                w_free = [list(begin), list(begin)]
                raw = Ring([sbuf(sc, f"{tag}raw{i}", [P, D]) for i in range(2)], begin)
                v = sbuf(sc, f"{tag}v", [P, ST, kv_heads, VW], BF16)
                k_st = sbuf(sc, f"{tag}kst", [P, HPG, SEQ], F32R)
                q_st = sbuf(sc, f"{tag}qst", [P, HPG, SEQ], F32R)
                k_free = [list(begin) for _ in range(HPG)]
                q_free = [list(begin) for _ in range(HPG)]
                stage = {n: [sbuf(sc, f"{tag}{n}s{p}", [P, SEQ], F32R) for p in range(2)]
                         for n in "qk"}
                stage_free = {n: list(begin) for n in "qk"}
                y = sbuf(sc, f"{tag}y", [P, ST, D])
                den = sbuf(sc, f"{tag}den", [P, ST, HEADS])
                y_free = list(begin)
                negmax = sbuf(sc, f"{tag}negmax", [P, ST])
                mcol = Ring([sbuf(sc, f"{tag}mcol{i}", [P, 2 * ST]) for i in range(2)], begin)
                mrow = Ring([sbuf(sc, f"{tag}mrow{i}", [2 * ST, P]) for i in range(2)], begin)
                const_in = []
                if bias:
                    rope_d, bq_d, bk_d, bv_d, bo_d = bias
                    rope = {n: sbuf(sc, f"{tag}rope{n}", [P, SEQ]) for n in "qk"}
                    bcol = sbuf(sc, f"{tag}bcol", [P, 4 + 1 + 1])
                    bo = sbuf(sc, f"{tag}bo", [P, D])
                    sp.dma(rope["q"][:], rope_d[0], begin, mark=S("bias"))
                    sp.dma(rope["k"][:], rope_d[1], mark=S("bias"))
                    sp.dma(bcol[:, 0:4], bq_d, mark=S("bias"))
                    sp.dma(bcol[:, 4:5], bk_d, mark=S("bias"))
                    sp.dma(bcol[:, 5:6], bv_d, mark=S("bias"))
                    const_in = [sp.dma(bo[:], bo_d, mark=S("bias"))]

                ones = pool.do(lambda e: e.memset(v[:, :, :, 0:1], 1.0), begin, mark=S("ones"))
                for j in range(HPG):
                    kones = dve.do(lambda e, j=j: e.memset(k_st[3 * HD:3 * HD + 2, j, :].bitcast(F32),
                                                            1.0), begin, mark=S("k_ones"))

                def load_pieces(names, slot, at=0):
                    toks = []
                    for n, (name, dst) in enumerate(names):
                        i, rb, r_free = raw.take()
                        landed = sp.dma(rb[:], name, r_free, mark=S(f"raw{i}"))
                        hi = pool.do(lambda e, d=dst, r=rb: e.tensor_copy(d[HI], r[:]), landed,
                                     w_free[slot], mark=S("w_hi"))
                        lo = pool.do(lambda e, d=dst, r=rb: e.tensor_tensor(
                            d[LO], r[:], d[HI].bitcast(F32), ALU.subtract), hi, w_free[1 - slot],
                            mark=S("w_lo"))
                        r_free[:] = [lo]
                        toks += [hi, lo]
                    return toks

                def wide(pieces):
                    return load_pieces([(pieces[k], (wbuf[:, 0, k, :], wbuf[:, 1, k, :]))
                                        for k in range(KT)], 0)

                def narrow(q_piece, k_piece, slot):
                    pcs = [(q_piece, (wbuf[:, slot, 0, :], wbuf[:, slot, 1, :]))]
                    if k_piece is not None:
                        pcs.append((k_piece, (wbuf[:, slot, 2, :], wbuf[:, slot, 3, :])))
                    hi_lo = []
                    for name, dst in pcs:
                        i, rb, r_free = raw.take()
                        landed = sp.dma(rb[:], name, r_free, mark=S(f"raw{i}"))
                        hi = pool.do(lambda e, d=dst, r=rb: e.tensor_copy(d[HI], r[:]), landed,
                                     w_free[slot], mark=S("w_hi"))
                        lo = pool.do(lambda e, d=dst, r=rb: e.tensor_tensor(
                            d[LO], r[:], d[HI].bitcast(F32), ALU.subtract), hi, mark=S("w_lo"))
                        r_free[:] = [lo]
                        hi_lo += [hi, lo]
                    return hi_lo

                def project(slot, at, c, *needs):
                    ps, ps_free = slots.take()
                    wv = [wbuf[:, slot, at + p, :].rearrange("p (k m) -> p k m", k=KT)
                          for p in range(2)]
                    terms = [(wv[wp][:, k, :], hA[hp][:, k, c * CH:(c + 1) * CH])
                             for k in range(KT) for wp, hp in THREE]
                    t = passes(ps[:, 0, :], terms, ps_free, *needs, mark=S("proj"))
                    return ps, ps_free, t

                def stage_piece(n, g, slot, at, c, *needs):
                    ps, ps_free, t = project(slot, at, c, *needs)
                    dst = [q[:, c * CH:(c + 1) * CH] for q in stage[n]]
                    return t, lambda: stage_split(n, g, c, ps, ps_free, dst, t)

                def stage_split(n, g, c, ps, ps_free, dst, t):
                    if not bias:
                        toks = split_psum(ps[:, 0, :], dst, t, stage_free[n], ps_free, "qk",
                                          scale=scale if n == "q" else None)
                    else:
                        _, buf, free = tmps.take()
                        col = bcol[:, g:g + 1] if n == "q" else bcol[:, 4:5]
                        rp = rope[n][:, c * CH:(c + 1) * CH]
                        r = dve.do(lambda e: e.scalar_tensor_tensor(
                            buf[:], ps[:, 0, :], col, rp, ALU.add, ALU.mult), t, free, const_in,
                            mark=S("rope"))
                        ps_free[:] = [r]
                        hi = act.do(lambda e: e.activation(dst[HI], buf[:], ACT.Copy), r,
                                    stage_free[n], mark=S("qk_hi"))
                        lo = dve.do(lambda e: e.tensor_tensor(dst[LO], buf[:], dst[HI].bitcast(F32),
                                                              ALU.subtract), hi, stage_free[n],
                                    mark=S("qk_lo"))
                        free[:] = [lo]
                        toks = [hi, lo]
                    return toks

                def stack(n, j, ready):
                    st, free = (q_st, q_free) if n == "q" else (k_st, k_free)
                    order = (HI, LO, HI) if n == "q" else (HI, HI, LO)
                    for r, part in enumerate(order):
                        t = sp.dma(st[r * HD:(r + 1) * HD, j, :].bitcast(F32),
                                   stage[n][part][j * HD:(j + 1) * HD, :].bitcast(F32),
                                   ready, free[j], mark=S(f"{n}_st{j}"))
                    return t

                def v_split(t, src, heads, ready, src_free):
                    n = heads * HD
                    part = [v[:, t, :, 1 + i * HD:1 + (i + 1) * HD] for i in range(3)]
                    s = src.rearrange("p (h d) -> p h d", d=HD)
                    v1 = act.do(lambda e: e.activation(part[0], s, ACT.Copy), ready, v_free,
                                mark=S("v1"))
                    _, buf, free = tmps.take()
                    r = buf[:, 0:n].rearrange("p (h d) -> p h d", d=HD)
                    r1 = dve.do(lambda e: e.tensor_tensor(r, s, part[0], ALU.subtract), v1, free,
                                mark=S("v_rest"))
                    src_free[:] = [r1]
                    v2 = act.do(lambda e: e.activation(part[1], r, ACT.Copy), r1, v_free,
                                mark=S("v2"))
                    v3 = dve.do(lambda e: e.tensor_tensor(part[2], r, part[1], ALU.subtract), v2,
                                v_free, mark=S("v3"))
                    free[:] = [v3]
                    return [v1, v2, v3]

                v_free = []
                for b in range(BATCH):
                    wv_in = wide(wd["v"]) if not grouped else narrow(wd["v"][0], wd["k"][0], 0)
                    h_in = []
                    for c in range(2):
                        rs = norm_stats(b * 2 + c)
                        for i in range(CT):
                            h_in += norm_tile(b * ST + c * CT + i, rs, hA, (c * CT + i) * P,
                                              hA_free[c])
                    if bias:
                        for t in range(b * ST, (b + 1) * ST):
                            x_ready[t] = pool.do(lambda e, t=t: e.tensor_tensor(
                                x[:, t, :], x[:, t, :], bo[:], ALU.add), S_last["rstd"],
                                x_ready[t], const_in, mark=S("x_pool"))

                    v_in = []
                    if grouped:
                        for c in range(2):
                            ps, ps_free, t = project(0, 0, c, wv_in, h_in)
                            _, buf, free = tmps.take()
                            vb = act.do(lambda e, ps=ps, buf=buf: e.activation(
                                buf[:], ps[:, 0, :], ACT.Identity, bias=bcol[:, 5:6]), t, free,
                                const_in, mark=S("v_bias"))
                            ps_free[:] = [vb]
                            ps2, ps2_free = slots.take()
                            pe.need(vb, ps2_free)
                            for i in range(CT):
                                tp = pe.do(lambda e, i=i, ps2=ps2, buf=buf: e.transpose(
                                    ps2[:, 0, i * P:(i + 1) * P], buf[:, i * P:(i + 1) * P],
                                    ident[:]), mark=S("v_tp"))
                            free[:] = [tp]
                            for i in range(CT):
                                v_in += v_split(c * CT + i, ps2[:, 0, i * P:(i + 1) * P], kv_heads,
                                                tp, ps2_free)
                        kt, k_toks = [], []
                        for c in range(2):
                            t, split = stage_piece("k", 0, 0, 2, c, wv_in, h_in)
                            k_toks += split()
                        w_free[0][:] = [t]
                        k_in = [stack("k", j, k_toks) for j in range(HPG)]
                        stage_free["k"][:] = list(k_in)
                    else:
                        for t in range(ST):
                            ps, ps_free = slots.take()
                            terms = [(hA[hp][:, k, t * P:(t + 1) * P], wbuf[:, wp, k, :])
                                     for k in range(KT) for wp, hp in THREE]
                            tok = passes(ps[:, 0, :], terms, ps_free, wv_in, h_in, mark=S("v_mm"))
                            v_in += v_split(t, ps[:, 0, :], kv_heads, tok, ps_free)
                        w_free[0][:] = [tok]
                        w_free[1][:] = [tok]
                        k_in = [None] * HPG
                    q_in = [None] * HPG
                    q_toks, k_toks2, w_g = [], [], {}

                    def group_weights(g):
                        w_g[g] = narrow(wd["q"][g], None if grouped else wd["k"][g], g % 2)

                    def group_piece(g, i):
                        n, c = ("q", "k")[i // 2], i % 2
                        if n == "k" and grouped:
                            return
                        if i == 0:
                            q_toks.clear()
                            k_toks2.clear()
                        t, split = stage_piece(n, g, g % 2, 0 if n == "q" else 2, c, w_g[g], h_in)
                        toks = q_toks if n == "q" else k_toks2
                        late.append(lambda: toks.extend(split()))
                        w_free[g % 2][:] = [t]
                        hA_free[c][:] = [t]

                    def stack_head(j):
                        q_in[j] = stack("q", j, list(q_toks))
                        stage_free["q"][:] = stage_free["q"][-3:] + [q_in[j]]
                        if not grouped:
                            k_in[j] = stack("k", j, list(k_toks2))
                            stage_free["k"][:] = stage_free["k"][-3:] + [k_in[j]]

                    def halves(ps, width):
                        return ps[:, 0:1, 0:width] if width <= CH else ps[:, :, 0:width // 2]

                    def head_of(n):
                        g, j = n // HPG, n % HPG
                        return (HPG * j + g, j, j) if grouped else (n, j, n)

                    def row_max(n, i):
                        _, j, _ = head_of(n)
                        w_ = (i + 1) * P
                        cols = max(w_, 2 * P)
                        pieces = 1 if cols <= CH else 2
                        ps, ps_free = slots.take(pieces)
                        pe.need(ps_free, q_in[j], k_in[j], consts)
                        pw = cols // pieces
                        for z in range(pieces):
                            pe.do(mm(ps[:, z, 0:pw], q_st[0:3 * HD, j, i * P:(i + 1) * P],
                                     k_st[0:3 * HD, j, z * pw:(z + 1) * pw], True, True))
                        end = w_ - (pieces - 1) * pw
                        t = pe.do(mm(ps[:, pieces - 1, end - P:end], ident_b[:], mask_q[:], False,
                                     True, True), mark=S("s_q"))
                        mx = dve.do(lambda e: e.tensor_reduce(
                            negmax[:, i:i + 1], halves(ps, w_), AX.XY, ALU.max, negate=True), t,
                            S_last.get("negmax"), mark=S("row_max"))
                        ps_free[:] = [mx]
                        return mx

                    def max_rows(n, mx):
                        _, j, _ = head_of(n)
                        _, mc, mc_free = mcol.take()
                        hi = dve.do(lambda e: e.tensor_copy(mc[:, 0:ST].bitcast(F32R), negmax[:]),
                                    mx, mc_free, mark=S("m_split"))
                        lo = dve.do(lambda e: e.tensor_tensor(mc[:, ST:2 * ST], negmax[:],
                                                              mc[:, 0:ST], ALU.subtract), hi,
                                    mark=S("m_split"))
                        S_last["negmax"] = lo
                        return n, j, mc, mc_free, lo

                    def turn_max(n, j, mc, mc_free, lo):
                        ps, ps_free = slots.take()
                        tp = pe.do(lambda e: e.transpose(ps[0:2 * ST, 0, 0:P], mc[:], ident[:]),
                                   lo, ps_free, mark=S("m_tp"))
                        mc_free[:] = [tp]
                        i, mr, mr_free = mrow.take()
                        cp = act.do(lambda e: e.activation(mr[:], ps[0:2 * ST, 0, 0:P], ACT.Copy),
                                    tp, mr_free, mark=S("m_row"))
                        ps_free[:] = [cp]
                        for r in range(2):
                            row = q_st[3 * HD + r:3 * HD + r + 1, j, :].bitcast(F32)
                            t = sp.dma(row.rearrange("o (i q) -> o i q", q=P),
                                       mr[r * ST:(r + 1) * ST, :], cp, q_free[j],
                                       mark=S(f"m_in{n % 2}"))
                        mr_free[:] = [t]
                        m_in[n] = t

                    def exp_keys(n, jt, m_in):
                        head, j, kv = head_of(n)
                        w_ = SEQ - jt * P
                        cols = max(w_, 2 * P)
                        pieces = 1 if cols <= CH else 2
                        pw, q0 = cols // pieces, SEQ - cols
                        skip = cols - w_
                        ps, ps_free = slots.take(pieces)
                        pe.need(ps_free, m_in, kones)
                        for z in range(pieces):
                            pe.do(mm(ps[:, z, 0:pw], k_st[0:3 * HD + 2, j, jt * P:(jt + 1) * P],
                                     q_st[0:3 * HD + 2, j, q0 + z * pw:q0 + (z + 1) * pw],
                                     True, True))
                        t = pe.do(mm(ps[:, 0, skip:skip + P], ident_b[:], mask_k[:], False, True,
                                     True), mark=S("s_k"))
                        if jt == ST - 1:
                            q_free[j][:] = [t]
                            if not grouped or n // HPG == HPG - 1:
                                k_free[j][:] = [t]
                        _, e_, e_free = e32.take()
                        src = halves(ps, w_) if pieces == 2 else ps[:, 0:1, skip:skip + w_]
                        dst = e_[:, 0:w_].rearrange("p (z w) -> p z w", z=pieces)
                        ex = act.do(lambda e: e.activation(dst, src, ACT.Exp, bias=p_scale[:]),
                                    t, e_free, consts, mark=S("exp"))
                        ps_free[:] = [ex]
                        _, (eh, el), e16_free = e16.take()
                        hi = None
                        if jt in HI_ON_ACT:
                            hi = act.do(lambda e: e.activation(
                                eh[:, 0:w_].rearrange("p (z w) -> p z w", z=pieces), src, ACT.Exp,
                                bias=p_scale[:]), e16_free, mark=S("p_hi_act"))
                            ps_free[:] = [hi]
                        return n, jt, w_, e_, e_free, ex, eh, el, e16_free, hi

                    def split_exp(n, jt, w_, e_, e_free, ex, eh, el, e16_free, hi):
                        if hi is None:
                            hi = dve.do(lambda e: e.tensor_copy(eh[:, 0:w_], e_[:, 0:w_]), ex,
                                        e16_free, mark=S("p_hi_dve"))
                        lane, nm = (pool, "p_lo_pool") if jt in LO_ON_POOL else (dve, "p_lo_dve")
                        lo = lane.do(lambda e: e.tensor_tensor(el[:, 0:w_], e_[:, 0:w_],
                                                               eh[:, 0:w_], ALU.subtract), hi,
                                     e16_free, mark=S(nm))
                        e_free[:] = [lo]
                        return n, jt, eh, el, [hi, lo], e16_free

                    acc_free = banks.free

                    def times_v(n, jt, eh, el, ready, e16_free):
                        head, _, kv = head_of(n)
                        pe.need(ready, v_in, ones)
                        if jt == 0:
                            pe.need(acc_free[0], acc_free[1])
                        for i in range(jt, ST):
                            o = acc[:, i // CT, i % CT * VW:i % CT * VW + 1 + 3 * HD]
                            q = slice((i - jt) * P, (i - jt + 1) * P)
                            first = jt == 0 and i % CT == 0
                            pe.do(mm(o, eh[:, q], v[:, jt, kv, 0:1 + 3 * HD], first, False, True))
                            t = pe.do(mm(o[:, 0:1 + 2 * HD], el[:, q], v[:, jt, kv, 0:1 + 2 * HD],
                                         False, i == jt, True),
                                      mark=S("pv") if i in (CT - 1, ST - 1) or i == jt else None)
                            if i == jt and i in (CT - 1, ST - 1):
                                take_y(n, i // CT, t)
                        e16_free[:] = [t]

                    def take_y(n, bank, t):
                        head, _, _ = head_of(n)
                        o = acc[:, bank, 0:CT * VW].rearrange("p (i w) -> p i w", w=VW)
                        parts = o[:, :, 1:1 + 3 * HD].rearrange("p i (s d) -> p i d s", s=3)
                        i0 = bank * CT
                        dve.do(lambda e: e.tensor_reduce(
                            y[:, i0:i0 + CT, head * HD:(head + 1) * HD], parts, AX.X, ALU.add), t,
                            y_free, mark=S("y_take"))
                        r = dve.do(lambda e: e.tensor_copy(den[:, i0:i0 + CT, head:head + 1],
                                                           o[:, :, 0:1]), t, y_free,
                                   mark=S("y_take"))
                        acc_free[bank][:] = [r]
                        taken[0] = r

                    taken = [None]
                    heads_sc = sc.enter_context(ExitStack())
                    now = ends()
                    e32 = Ring([sbuf(heads_sc, f"{tag}e{b}{i}", [P, SEQ]) for i in range(3)], now)
                    e16 = Ring([[sbuf(heads_sc, f"{tag}e{b}{p}{i}", [P, SEQ], F16)
                                 for p in range(2)] for i in range(4)], now)
                    group_weights(0)
                    group_weights(1)
                    late = []
                    for i in range(4):
                        group_piece(0, i)
                    for step in late:
                        step()
                    late.clear()
                    for j in range(HPG):
                        stack_head(j)
                    m_in = {}

                    def row_unit(u):
                        n, i = divmod(u, ST)
                        if n < HEADS:
                            mx = row_max(n, (u - AHEAD) % ST)
                            if i == ST - 1:
                                late.append(lambda m=max_rows(n, mx): turn_max(*m))

                    for u in range(AHEAD):
                        row_unit(u)
                    late.pop()()
                    fresh, behind = [], []
                    for n in range(HEADS):
                        g, j = divmod(n, HPG)
                        for s in range(ST):
                            put_off, late[:] = late[:], []
                            row_unit(n * ST + s + AHEAD)
                            fresh.append(exp_keys(n, s, m_in[n]))
                            if len(fresh) > 1:
                                behind.append(split_exp(*fresh.pop(0)))
                            if len(behind) > 2:
                                times_v(*behind.pop(0))
                            for step in put_off:
                                step()
                            if j == 0 and g + 1 < HPG and s % 2 == 1:
                                group_piece(g + 1, s // 2)
                        while late and j == 0:
                            late.pop(0)()
                        if g + 1 < HPG:
                            stack_head(j)
                        if j == 1 and g + 2 < HPG:
                            group_weights(g + 2)
                    wo_in = wide(wd["o"])
                    behind.append(split_exp(*fresh.pop()))
                    for u in behind:
                        times_v(*u)
                    v_free[:] = [pe.last]

                    heads_sc.close()
                    proj_sc = sc.enter_context(ExitStack())
                    now = ends()
                    yT = Ring([[sbuf(proj_sc, f"{tag}yT{b}{i}{p}", [P, KT, P], F32R)
                                for p in range(2)] for i in range(2)], now)
                    rec = dve.do(lambda e: e.reciprocal(den[:], den[:]), taken[0], mark=S("recip"))
                    for t in range(ST):
                        yn = pool.do(lambda e, t=t: e.tensor_tensor(
                            y[:, t, :].rearrange("p (h d) -> p h d", d=HD),
                            y[:, t, :].rearrange("p (h d) -> p h d", d=HD),
                            den[:, t, :].unsqueeze(2).to_broadcast([P, HEADS, HD]), ALU.mult), rec,
                            mark=S("y_norm"))
                        ps, ps_free = slots.take()
                        pe.need(yn, ps_free)
                        for k in range(KT):
                            tp = pe.do(lambda e, k=k, t=t, ps=ps: e.transpose(
                                ps[:, 0, k * P:(k + 1) * P], y[:, t, k * P:(k + 1) * P], ident[:]),
                                mark=S("y_tp") if k == KT - 1 else None)
                        src = ps[:, 0, :].rearrange("p (k q) -> p k q", k=KT)
                        _, yt, yT_free = yT.take()
                        toks = split_psum(src, [q[:] for q in yt], tp, yT_free, ps_free, "y")
                        y_free[:] = [tp]
                        i, bank, free = banks.take()
                        terms = [(yt[yp][:, k, :], wbuf[:, wp, k, :])
                                 for k in range(KT) for wp, yp in THREE]
                        o = passes(bank, terms, free, toks, wo_in, mark=S("o_proj"))
                        yT_free[:] = [o]
                        tt = b * ST + t
                        x_ready[tt] = dve.do(lambda e, tt=tt, bank=bank: e.tensor_tensor(
                            x[:, tt, :], bank, x[:, tt, :], ALU.add), o, x_ready[tt],
                            S_last["rstd"], mark=S("x_add"))
                        free[:] = [x_ready[tt]]
                    w_free[0][:] = [o]
                    w_free[1][:] = [o]
                    proj_sc.close()

        AHEAD = 13
        HI_ON_ACT = (1, 3, 6)
        LO_ON_POOL = (0, 2, 4, 5, 7)

        ffn0 = ("f0", a["gate0"], a["up0"], a["down0"], 1536, 384,
                (a["gscale"], a["uscale"], a["dscale"].partition_broadcast(P)), True)
        ffn1 = ("f1", a["gate1"], a["up1"], a["down1"], 2048, 256, None, False)
        score_scale = float(1.0 / np.sqrt(np.float32(HD)))
        w0 = {n: [a[n + "0"][i] for i in range(k)] for n, k in
              (("q", 4), ("k", 1), ("v", 1), ("o", 4))}
        w1 = {n: [a[n + "1"][i] for i in range(4)] for n in "qkvo"}
        for s in STAGES:
            if s == "f0":
                ffn(ffn0[0] + str(len(sems)), *ffn0[1:])
            elif s == "f1":
                ffn(ffn1[0] + str(len(sems)), *ffn1[1:])
            elif s == "a0":
                attention("a0", w0, KV0, score_scale,
                          (a["rope"], a["bq"], a["bk"], a["bv"], a["bo"].partition_broadcast(P)))
            else:
                attention("a1", w1, HEADS, score_scale)

        out_rows = out.rearrange("(t p) d -> t p d", p=P)
        for t in range(NT):
            done = sp.dma(out_rows[t], x[:, t, :], x_ready[t], mark=S("out"))
        sp.need(done)

        with nc.Block() as block:
            block.sync(sp.play)
            block.tensor(pe.play)
            block.scalar(act.play)
            block.vector(dve.play)
            block.gpsimd(pool.play)


STAGES = ("f0", "a0", "f0", "f1", "a1", "f1")


def rope_table():
    inv = np.float32(10000.0) ** (np.float32(-2.0) * np.arange(HD // 2, dtype=np.float32)
                                  / np.float32(HD))
    theta = np.arange(SEQ, dtype=np.float32)[:, None] * inv[None, :]
    table = np.tile((np.cos(theta) + np.sin(theta)).T, (2 * HPG, 1)).astype(np.float32)
    return np.stack([table / np.sqrt(np.float32(HD)), table]).astype(np.float32)


def layouts(i):
    def gate(w, gw):
        n = w.shape[1] // gw
        return w.reshape(KT, P, n, gw).transpose(2, 1, 0, 3).reshape(n, P, KT * gw)

    def down(w, gw):
        n = w.shape[0] // gw
        return w.reshape(n, gw // P, P, D).transpose(0, 2, 1, 3).reshape(n, P, gw // P * D)

    def cols(w):
        n = w.shape[1] // P
        return w.reshape(KT, P, n, P).transpose(2, 1, 0, 3).reshape(n, P, KT * P)

    def rows(w):
        return w.reshape(KT, P, D)

    def regroup(w):
        return w.reshape(*w.shape[:-1], HPG, HPG, HD).swapaxes(-3, -2).reshape(w.shape)

    wa = i["L1_attn_w_attn"]
    return {
        "x": i["L0_attn_x"].reshape(TOK, D),
        "gate0": gate(i["L0_ffn_gate_w"], 384), "up0": gate(i["L0_ffn_up_w"], 384),
        "down0": down(i["L0_ffn_down_w"], 384),
        "gscale": i["L0_ffn_gate_scale"].reshape(-1, P).T,
        "uscale": i["L0_ffn_up_scale"].reshape(-1, P).T,
        "dscale": i["L0_ffn_down_scale"],
        "gate1": gate(i["L1_ffn_w_gate"].T, 256), "up1": gate(i["L1_ffn_w_up"].T, 256),
        "down1": down(i["L1_ffn_w_down"].T, 256),
        "q0": cols(regroup(i["L0_attn_Wq"].T)), "k0": cols(i["L0_attn_Wk"].T),
        "v0": cols(i["L0_attn_Wv"].T), "o0": rows(i["L0_attn_Wo"].T),
        "bq": regroup(i["L0_attn_bq"]).reshape(HPG, P).T, "bk": i["L0_attn_bk"].reshape(P, 1),
        "bv": i["L0_attn_bv"].reshape(P, 1), "bo": i["L0_attn_bo"],
        "q1": cols(wa[:, 0:D]), "k1": cols(wa[:, D:2 * D]), "v1": rows(wa[:, 2 * D:3 * D]),
        "o1": rows(i["L1_attn_w_proj"]),
        "rope": rope_table(),
    }


def kernel(**inputs):
    import concourse.bacc as bacc
    from concourse.bass_utils import run_bass_kernel_spmd

    arrays = {f"in_{n}": np.ascontiguousarray(v) for n, v in
              layouts({n: np.asarray(v) for n, v in inputs.items()}).items()}
    nc = bacc.Bacc("TRN2", target_bir_lowering=False, num_devices=1)
    aps = {n[3:]: nc.dram_tensor(n, v.shape, F32, kind="ExternalInput").ap() for n, v in arrays.items()}
    out = nc.dram_tensor("out", (TOK, D), F32, kind="ExternalOutput").ap()
    build(nc, aps, out)
    r = run_bass_kernel_spmd(nc, [arrays], core_ids=[0])
    return r.results[0]["out"].reshape(BATCH, SEQ, D)
```

```python
from contextlib import ExitStack

import numpy as np

import concourse.bass as bass
from concourse import mybir

F32 = mybir.dt.float32
F32R = mybir.dt.float32r
F16 = mybir.dt.float16
BF16 = mybir.dt.bfloat16
FP8 = mybir.dt.float8e4
ALU = mybir.AluOpType
ACT = mybir.ActivationFunctionType
AX = mybir.AxisListType

P = 128
BATCH, SEQ, D = 2, 1024, 512
TOK = BATCH * SEQ
NT = TOK // P
ST = SEQ // P
KT = D // P
CH = 512
NC = TOK // CH
CT = CH // P
HEADS, HD = 16, 32
HPG = P // HD
KV0 = 4
VW = 98
EPS = 1e-5
MASKED = -1e30
FP8_TRN_MAX = 240.0
FP8_FN_MAX = 448.0
NAN_SCALE = 3.4e38 / 464.0
P_SCALE_LN = float(np.log(1024.0))


class Lane:

    def __init__(self, name):
        self.name, self.ops, self.seen, self.last = name, [], {}, None

    def need(self, *tokens):
        for t in tokens:
            if isinstance(t, list):
                self.need(*t)
            elif t is not None and self.seen.get(t[0].name, 0) < t[1]:
                self.seen[t[0].name] = t[1]
                self.ops.append((None, t[0].handle, t[1]))

    def do(self, emit, *tokens, mark=None):
        self.need(*tokens)
        token = mark.up(1) if mark else None
        self.ops.append((emit, mark.handle if mark else None, 1))
        self.last = token
        return token

    def dma(self, out, in_, *tokens, mark):
        self.need(*tokens)
        token = mark.up(16)
        self.ops.append((lambda e, out=out, in_=in_: e.dma_start(out, in_), mark.handle, 16))
        return token

    def play(self, engine):
        for emit, sem, value in self.ops:
            if emit is None:
                engine.wait_ge(sem, value)
            else:
                ins = emit(engine)
                if sem is not None:
                    ins.then_inc(sem, value)


class Sem:
    def __init__(self, ctx, nc, name):
        self.name, self.handle, self.count = name, ctx.enter_context(nc.semaphore(name)), 0

    def up(self, by):
        self.count += by
        return self, self.count


class Readers(list):

    def __init__(self, tokens=()):
        super().__init__(tokens)
        self.in_use = False

    def __setitem__(self, key, tokens):
        super().__setitem__(key, tokens)
        self.in_use = False

    def hand_out(self):
        assert not self.in_use
        self.in_use = True
        return self


class Ring:

    def __init__(self, views, free=()):
        self.views, self.free, self.at = views, [Readers(free) for _ in views], 0

    def take(self):
        i = self.at % len(self.views)
        self.at += 1
        return i, self.views[i], self.free[i].hand_out()


class Banks:

    def __init__(self, view):
        self.view, self.n = view, view.shape[1]
        self.free, self.at = [Readers() for _ in range(self.n)], 0

    def take(self, width=1):
        if self.at + width > self.n:
            self.at = 0
        i = self.at
        self.at = (i + width) % self.n
        assert not any(f.in_use for f in self.free[i:i + width])
        free = Readers([t for f in self.free[i:i + width] for t in f])
        for k in range(i, i + width):
            self.free[k] = free
        return self.view[:, i:i + width, :], free.hand_out()


class Jobs:

    def __init__(self):
        self.waiting, self.running = [], []

    def tick(self, start=True):
        self.running = [job for job in self.running if next(job, "done") != "done"]
        if start and self.waiting:
            self.start(self.waiting.pop(0))

    def start(self, job):
        if next(job, "done") != "done":
            self.running.append(job)

    def finish(self, job):
        while job in self.waiting or job in self.running:
            self.tick()

    def flush(self):
        while self.waiting or self.running:
            self.tick()


def build(nc, a, out):
    with ExitStack() as ctx:
        pe, act, dve, pool, sp = (Lane(n) for n in ("pe", "act", "dve", "pool", "sp"))
        sems = {}

        def S(name):
            if name not in sems:
                sems[name] = Sem(ctx, nc, name)
            return sems[name]

        def sbuf(scope, name, shape, dt=F32):
            return scope.enter_context(nc.sbuf_tensor(name, shape, dt))

        x = sbuf(ctx, "x", [P, NT, D])
        hA = [sbuf(ctx, f"hA_{p}", [P, KT, SEQ], F32R) for p in ("hi", "lo")]
        ident = sbuf(ctx, "ident", [P, P])
        ident_b = sbuf(ctx, "ident_b", [P, P], BF16)
        mask_q = sbuf(ctx, "mask_q", [P, P], BF16)
        mask_k = sbuf(ctx, "mask_k", [P, P], BF16)
        stats = sbuf(ctx, "stats", [P, CT, 6])
        meanvar = sbuf(ctx, "meanvar", [P, NT, 2])
        rstd = sbuf(ctx, "rstd", [P, NT])
        minus_half = sbuf(ctx, "minus_half", [P, CT])
        p_scale = sbuf(ctx, "p_scale", [P, 1])
        tmp = [sbuf(ctx, f"tmp{i}", [P, D]) for i in range(2)]
        raw = Ring([sbuf(ctx, f"raw{i}", [P, D]) for i in range(2)])
        wmem = sbuf(ctx, "wmem", [P, 2, 4, D], F32R)

        psum = ctx.enter_context(nc.psum_tensor("psum", [P, 6, 512], F32))
        acc = ctx.enter_context(nc.psum_tensor("acc", [P, 2, 512], F32))
        slots = Banks(psum[:, :, :])
        banks = Ring([acc[:, 0, :], acc[:, 1, :]])
        tmps = Ring(tmp)

        c0 = pool.do(lambda e: e.memset(ident[:], 0.0), mark=S("const"))
        c1 = pool.do(lambda e: e.memset(ident_b[:], 0.0), mark=S("const"))
        c2 = pool.do(lambda e: e.memset(mask_q[:], 0.0), mark=S("const"))
        c3 = pool.do(lambda e: e.memset(mask_k[:], 0.0), mark=S("const"))
        pool.do(lambda e: e.memset(minus_half[:], -0.5), mark=S("const"))
        pool.do(lambda e: e.memset(p_scale[:], P_SCALE_LN), mark=S("const"))
        for t in (ident, ident_b):
            pool.do(lambda e, t=t: e.affine_select(
                out=t[:], in_=t[:], compare_op=ALU.not_equal, fill=1.0, base=0,
                pattern=[[-1, P]], channel_multiplier=1), c0, c1, c2, c3, mark=S("const"))
        pool.do(lambda e: e.affine_select(
            out=mask_q[:], in_=mask_q[:], compare_op=ALU.is_ge, fill=MASKED, base=0,
            pattern=[[-1, P]], channel_multiplier=1), mark=S("const"))
        consts = pool.do(lambda e: e.affine_select(
            out=mask_k[:], in_=mask_k[:], compare_op=ALU.is_ge, fill=MASKED, base=0,
            pattern=[[1, P]], channel_multiplier=-1), mark=S("const"))

        x_rows = a["x"].rearrange("(t p) d -> t p d", p=P)
        x_ready = [sp.dma(x[:, t, :], x_rows[t], mark=S(f"x_in{t // CT}")) for t in range(NT)]
        x_ready = [x_ready[t // CT * CT + CT - 1] for t in range(NT)]
        x_read = [None] * NT

        def mm(out_, lhsT, rhs, start, stop, skip=False):
            return lambda e: e.matmul(out_, lhsT, rhs, start=start, stop=stop,
                                      skip_group_check=skip)

        def passes(out_, terms, *tokens, mark=None):
            pe.need(*tokens)
            for n, (w, m) in enumerate(terms):
                last = n == len(terms) - 1
                t = pe.do(mm(out_, w, m, n == 0, last), mark=mark if last else None)
            return t

        HI, LO = 0, 1
        THREE = ((HI, HI), (HI, LO), (LO, HI))

        def norm_stats(c):
            for i in range(CT):
                t = c * CT + i
                st = dve.do(lambda e, i=i, t=t: e.bn_stats(stats[:, i, :], x[:, t, :]),
                            x_ready[t], S_last.get("stats"), mark=S("ln_stats"))
            for i in range(CT):
                t = c * CT + i
                ag = dve.do(lambda e, i=i, t=t: e.bn_aggr(meanvar[:, t, :], stats[:, i, :]),
                            st, mark=S("ln_stats"))
            S_last["stats"] = ag
            tiles = slice(c * CT, (c + 1) * CT)
            ve = pool.do(lambda e: e.tensor_scalar(rstd[:, tiles], meanvar[:, tiles, 1], EPS, None,
                                                   ALU.add), ag, S_last.get("rstd"), mark=S("ln_rstd"))
            rs = pool.do(lambda e: e.tensor_tensor(rstd[:, tiles], rstd[:, tiles], minus_half[:],
                                                   ALU.pow), ve, consts, mark=S("ln_rstd"))
            return rs

        S_last = {}

        def norm_jobs(c, h, h_free, toks):
            rs = []

            def stats_job():
                rs.append(norm_stats(c))
                yield

            def tile_job(i):
                t, at = c * CT + i, i * P
                _, buf, free = tmps.take()
                hn = dve.do(lambda e: e.tensor_scalar(buf[:], x[:, t, :], meanvar[:, t, 0:1],
                                                      rstd[:, t:t + 1], ALU.subtract, ALU.mult),
                            rs[0], free, mark=S("ln_out"))
                S_last["rstd"] = hn
                yield
                ps, ps_free = slots.take()
                pe.need(hn, ps_free, consts)
                for k in range(KT):
                    tp = pe.do(lambda e, k=k: e.transpose(ps[:, 0, k * P:(k + 1) * P],
                                                          buf[:, k * P:(k + 1) * P], ident[:]),
                               mark=S("ln_tp") if k == KT - 1 else None)
                free[:] = [tp]
                src = ps[:, 0, :].rearrange("p (k q) -> p k q", k=KT)
                dst = [q[:, :, at:at + P] for q in h]
                hi = act.do(lambda e: e.activation(dst[HI], src, ACT.Copy), tp, h_free,
                            mark=S("ln_hi"))
                yield
                lo = dve.do(lambda e: e.tensor_tensor(dst[LO], src, dst[HI].bitcast(F32),
                                                      ALU.subtract), hi, h_free, mark=S("ln_lo"))
                ps_free[:] = [lo]
                toks.extend([hi, lo])
            return [stats_job()] + [tile_job(i) for i in range(CT)]

        def split_job(src, dst, free, toks):
            i, rb, r_free = raw.take()
            landed = sp.dma(rb[:], src, r_free, mark=S(f"raw{i}"))
            yield
            hi = act.do(lambda e: e.activation(dst[HI], rb[:], ACT.Copy), landed, free,
                        mark=S("w_hi"))
            lo = pool.do(lambda e: e.tensor_tensor(dst[LO], rb[:], dst[HI].bitcast(F32),
                                                   ALU.subtract), hi, free, mark=S("w_lo"))
            r_free[:] = [lo]
            toks.extend([hi, lo])

        def fp8_buffers(scope, tag, n):
            return Ring([([sbuf(scope, f"{tag}q8{i}{k}", [P, D], FP8) for k in range(2)],
                          [sbuf(scope, f"{tag}qb{i}{k}", [P, D], BF16) for k in range(3)],
                          sbuf(scope, f"{tag}qz{i}", [P, D])) for i in range(n)], ends())

        def round_job(src, dst, free, toks, buffers):
            i, rb, r_free = raw.take()
            landed = sp.dma(rb[:], src, r_free, mark=S(f"raw{i}"))
            yield
            _, (q8, qb, qz), q_free = buffers.take()
            one = act.do(lambda e: e.activation(q8[0][:], rb[:], ACT.Copy, saturate=False),
                         landed, q_free, mark=S("q8"))
            half = act.do(lambda e: e.activation(q8[1][:], rb[:], ACT.Copy, scale=0.5,
                                                 saturate=False), mark=S("q8"))
            r_free[:] = [half]
            yield
            m = FP8_TRN_MAX
            low = dve.do(lambda e: e.tensor_scalar(qb[0][:], q8[0][:], m, -m, ALU.min,
                                                   ALU.max), one, q_free, mark=S("q_dve"))
            clp = dve.do(lambda e: e.tensor_scalar(qb[1][:], q8[1][:], m / 2, -m / 2,
                                                   ALU.min, ALU.max), half, mark=S("q_dve"))
            over = pool.do(lambda e: e.tensor_tensor(qb[2][:], q8[1][:], qb[1][:],
                                                     ALU.subtract), clp, q_free,
                           mark=S("q_pool"))
            yield
            q = dve.do(lambda e: e.scalar_tensor_tensor(qb[0][:], qb[2][:], 2.0, qb[0][:],
                                                        ALU.mult, ALU.add), low, over,
                       mark=S("q_dve"))
            z = dve.do(lambda e: e.tensor_scalar(qz[:], qb[0][:], NAN_SCALE, 0.0, ALU.mult,
                                                 ALU.mult), q, q_free, mark=S("q_dve"))
            res = pool.do(lambda e: e.tensor_tensor(dst, qb[0][:], qz[:], ALU.add), z,
                          free, mark=S("q_pool"))
            q_free[:] = [res]
            toks.append(res)

        def split_psum(src, dst, ready, dst_free, src_free, tag, scale=None):
            hi = act.do(lambda e: e.activation(dst[HI], src, ACT.Copy,
                                               scale=1.0 if scale is None else scale),
                        ready, dst_free, mark=S(f"{tag}_hi"))
            hi32 = dst[HI].bitcast(F32)
            if scale is None:
                lo = dve.do(lambda e: e.tensor_tensor(dst[LO], src, hi32, ALU.subtract),
                            hi, dst_free, mark=S(f"{tag}_lo"))
            else:
                lo = dve.do(lambda e: e.scalar_tensor_tensor(dst[LO], src, scale, hi32, ALU.mult,
                                                             ALU.subtract),
                            hi, dst_free, mark=S(f"{tag}_lo"))
            src_free[:] = [lo]
            return [hi, lo]

        def ends():
            return [l.last for l in (pe, act, dve, pool) if l.last is not None]

        hA_free = [[] for _ in range(2)]
        hA_in = [[], []]
        wmem_in = []
        norms, weights = Jobs(), Jobs()

        def tick():
            norms.tick()
            weights.tick()

        def hA_norm(c, half):
            hA_in[half] = []
            h = [q[:, :, half * CH:(half + 1) * CH] for q in hA]
            norms.waiting += norm_jobs(c, h, hA_free[half], hA_in[half])

        def ffn_first_weights(gate_d, up_d, quantised, free, buffers):
            flat = wmem[:].rearrange("p a b d -> p (a b d)")
            jobs, at, toks = [], 0, []
            for src in (gate_d, up_d):
                pieces = src.shape[2] // D
                for i in range(pieces):
                    cols = src[0][:, i * D:(i + 1) * D]
                    if quantised:
                        jobs.append(round_job(cols, flat[:, at + i * D:at + (i + 1) * D], free,
                                              toks, buffers))
                    else:
                        lo = at + (pieces + i) * D
                        jobs.append(split_job(cols, [flat[:, at + i * D:at + (i + 1) * D],
                                                     flat[:, lo:lo + D]], free, toks))
                at += pieces * D * (1 if quantised else 2)
            wmem_in[:] = [toks]
            return jobs

        def ffn(tag, gate_d, up_d, down_d, hidden, gw, scales, quantised, then):
            with ExitStack() as sc:
                begin = ends()
                groups, MT = hidden // gw, gw // P
                parts = 1 if quantised else 2
                hB = [sbuf(sc, f"{tag}hB{p}", [P, KT, SEQ], F32R) for p in range(2)]
                h = [[q[:, :, c % 2 * CH:(c % 2 + 1) * CH] for q in (hA, hB)[c // 2]]
                     for c in range(NC)]
                h_free = [hA_free[0], hA_free[1], list(begin), list(begin)]
                wn = KT * gw
                flat = wmem[:].rearrange("p a b d -> p (a b d)")
                w = [[[flat[:, (n * parts + p) * wn:(n * parts + p + 1) * wn] if b == 0 and n < 2
                       else sbuf(sc, f"{tag}w{n}{b}{p}", [P, wn], F32R)[:] for p in range(parts)]
                      for n in range(3)] for b in range(2)]
                w_free = [list(begin), list(begin)]
                act_ = [[sbuf(sc, f"{tag}a{b}{p}", [P, MT, CH], F32R) for p in range(2)]
                        for b in range(2)]
                a_free = [list(begin), list(begin)]
                silu = Ring([sbuf(sc, f"{tag}silu{i}", [P, CH]) for i in range(2)], begin)
                prod = Ring([sbuf(sc, f"{tag}prod{i}", [P, CH]) for i in range(2)], begin)
                buffers = fp8_buffers(sc, tag, 3) if quantised else None
                if quantised:
                    gs = sbuf(sc, f"{tag}gs", [P, hidden // P])
                    us = sbuf(sc, f"{tag}us", [P, hidden // P])
                    ds = sbuf(sc, f"{tag}ds", [P, D])
                    dso = [sbuf(sc, f"{tag}dso{i}", [P, D]) for i in range(2)]
                    dso = Ring(dso, begin)
                    sp.dma(gs[:], scales[0], begin, mark=S("scales"))
                    sp.dma(us[:], scales[1], mark=S("scales"))
                    sc_in = sp.dma(ds[:], scales[2], mark=S("scales"))

                def load_weights(g, names=(0, 1, 2)):
                    b = g % 2
                    for n in names:
                        src, w_in[b][n] = (gate_d, up_d, down_d)[n], []
                        for i in range(wn // D):
                            cols = slice(i * D, (i + 1) * D)
                            dst = [q[:, cols] for q in w[b][n]]
                            if quantised:
                                job = round_job(src[g][:, cols], dst[0], w_free[b], w_in[b][n],
                                                buffers)
                            else:
                                job = split_job(src[g][:, cols], dst, w_free[b], w_in[b][n])
                            weights.waiting.append(job)

                def gate_up(g, c, n, w_in, h_in):
                    b, wb = n % 2, w[g % 2]
                    views = [[q.rearrange("p (k m) -> p k m", k=KT) for q in wb[i]]
                             for i in range(2)]
                    pairs = ((HI, HI), (HI, LO)) if quantised else THREE
                    done, late = [], None
                    for m in range(MT):
                        mt = g * MT + m
                        ps, ps_free = slots.take(2)
                        toks = []
                        for i in range(2):
                            terms = [(views[i][wp][:, k, m * P:(m + 1) * P], h[c][hp][:, k, :])
                                     for k in range(KT) for wp, hp in pairs]
                            toks.append(passes(ps[:, i, :], terms, ps_free, w_in[g % 2][i], h_in,
                                               mark=S("gate_up")))
                        _, s, s_free = silu.take()
                        _, pr, p_free = prod.take()
                        if quantised:
                            sl = act.do(lambda e, s=s, ps=ps, mt=mt: e.activation(
                                s[:], ps[:, 0, :], ACT.Silu, scale=gs[:, mt:mt + 1]),
                                toks[0], s_free, sc_in, mark=S("silu"))
                            pt = dve.do(lambda e, s=s, ps=ps, pr=pr, mt=mt: e.scalar_tensor_tensor(
                                pr[:], ps[:, 1, :], us[:, mt:mt + 1], s[:], ALU.mult, ALU.mult),
                                toks[1], sl, p_free, sc_in, mark=S("prod"))
                        else:
                            sl = act.do(lambda e, s=s, ps=ps: e.activation(
                                s[:], ps[:, 0, :], ACT.Silu), toks[0], s_free, mark=S("silu"))
                            pt = dve.do(lambda e, s=s, ps=ps, pr=pr: e.tensor_tensor(
                                pr[:], ps[:, 1, :], s[:], ALU.mult), toks[1], sl, p_free,
                                mark=S("prod"))
                        s_free[:] = [pt]
                        ps_free[:] = [sl, pt]
                        hi = act.do(lambda e, pr=pr, m=m: e.activation(
                            act_[b][HI][:, m, :], pr[:], ACT.Copy), pt, a_free[b], mark=S("a_hi"))
                        if late:
                            done.append(late())
                        tick()

                        def late(pr=pr, m=m, hi=hi, p_free=p_free):
                            lo = dve.do(lambda e: e.tensor_tensor(
                                act_[b][LO][:, m, :], pr[:], act_[b][HI][:, m, :].bitcast(F32),
                                ALU.subtract), hi, a_free[b], mark=S("a_lo"))
                            p_free[:] = [lo]
                            return lo
                    done.append(late())
                    h_free[c][:] = [toks[1]]
                    return [done[-1], hi]

                def down(g, c, n, a_in, w_in):
                    b = n % 2
                    wd = [q.rearrange("p (m d) -> p m d", m=MT) for q in w[g % 2][2]]
                    pairs = ((HI, HI), (LO, HI)) if quantised else THREE
                    for i in range(CT):
                        t = c * CT + i
                        _, bank, free = banks.take()
                        terms = [(act_[b][ap][:, m, i * P:(i + 1) * P], wd[wp][:, m, :])
                                 for m in range(MT) for ap, wp in pairs]
                        y = passes(bank, terms, free, a_in, w_in[g % 2][2], mark=S("down"))
                        if quantised:
                            _, o, o_free = dso.take()
                            ev = dve.do(lambda e, o=o, bank=bank: e.scalar_tensor_tensor(
                                o[:], bank, 0.5, ds[:], ALU.mult, ALU.mult), y, o_free, sc_in,
                                mark=S("x_add"))
                            x_ready[t] = pool.do(lambda e, t=t, o=o: e.tensor_tensor(
                                x[:, t, :], x[:, t, :], o[:], ALU.add), ev, x_ready[t], S_last.get("rstd"),
                                mark=S("x_pool"))
                            o_free[:] = [x_ready[t]]
                            free[:] = [ev]
                        else:
                            x_ready[t] = dve.do(lambda e, t=t, bank=bank: e.scalar_tensor_tensor(
                                x[:, t, :], bank, 0.5, x[:, t, :], ALU.mult, ALU.add), y,
                                x_ready[t], mark=S("x_add"))
                            free[:] = [x_ready[t]]
                        tick()
                    a_free[b][:] = [y]
                    w_free[g % 2][:] = [y]

                w_in = [[wmem_in[:], wmem_in[:], None], [None] * 3]
                load_weights(0, (2,))
                h_in = [hA_in[0], hA_in[1], [], []]
                normed = {}
                pending = None
                n = 0
                for g in range(groups):
                    for c in range(NC):
                        if g == 0 and c < 2:
                            jobs = norm_jobs(c + 2, h[c + 2], h_free[c + 2], h_in[c + 2])
                            norms.waiting += jobs
                            normed[c + 2] = jobs[-1]
                        if g == 0 and c > 1:
                            norms.finish(normed[c])
                        if c == 1 or c == 0 and g > 0:
                            weights.flush()
                        if c == 1 and g + 1 < groups:
                            load_weights(g + 1)
                        if g == groups - 1 and then:
                            if c == 1:
                                weights.waiting += then(w_free[0], buffers)
                            if c > 1:
                                hA_norm(c - 2, c - 2)
                        a_in = gate_up(g, c, n, w_in, h_in[c])
                        if pending:
                            down(*pending, w_in)
                        pending = (g, c, n, a_in)
                        n += 1
                down(*pending, w_in)
                weights.flush()
                norms.flush()

        def attention(tag, wd, kv_heads, scale, bias, then, then_fp8):
            grouped = kv_heads < HEADS
            with ExitStack() as sc:
                begin = ends()
                w_free = [[], []]
                buffers = fp8_buffers(sc, tag, 1) if then_fp8 else None
                v = sbuf(sc, f"{tag}v", [P, ST, kv_heads, VW], BF16)
                k_st = sbuf(sc, f"{tag}kst", [P, HPG, SEQ], F32R)
                q_st = sbuf(sc, f"{tag}qst", [P, HPG, SEQ], F32R)
                k_free = [list(begin) for _ in range(HPG)]
                q_free = [list(begin) for _ in range(HPG)]
                stage = {n: [sbuf(sc, f"{tag}{n}s{p}", [P, SEQ], F32R) for p in range(2)]
                         for n in "qk"}
                stage_free = {n: list(begin) for n in "qk"}
                y = sbuf(sc, f"{tag}y", [P, ST, D])
                den = sbuf(sc, f"{tag}den", [P, ST, HEADS])
                y_free = list(begin)
                negmax = sbuf(sc, f"{tag}negmax", [P, ST])
                mcol = Ring([sbuf(sc, f"{tag}mcol{i}", [P, 2 * ST]) for i in range(2)], begin)
                mrow = Ring([sbuf(sc, f"{tag}mrow{i}", [2 * ST, P]) for i in range(2)], begin)
                const_in = []
                if bias:
                    rope_d, bq_d, bk_d, bv_d, bo_d = bias
                    rope = {n: sbuf(sc, f"{tag}rope{n}", [P, SEQ]) for n in "qk"}
                    bcol = sbuf(sc, f"{tag}bcol", [P, 4 + 1 + 1])
                    bo = sbuf(sc, f"{tag}bo", [P, D])
                    sp.dma(rope["q"][:], rope_d[0], begin, mark=S("bias"))
                    sp.dma(rope["k"][:], rope_d[1], mark=S("bias"))
                    sp.dma(bcol[:, 0:4], bq_d, mark=S("bias"))
                    sp.dma(bcol[:, 4:5], bk_d, mark=S("bias"))
                    sp.dma(bcol[:, 5:6], bv_d, mark=S("bias"))
                    const_in = [sp.dma(bo[:], bo_d, mark=S("bias"))]

                ones = pool.do(lambda e: e.memset(v[:, :, :, 0:1], 1.0), begin, mark=S("ones"))
                cleared = ones
                for j in range(HPG):
                    for st in (q_st, k_st):
                        cleared = pool.do(lambda e, j=j, st=st: e.memset(
                            st[3 * HD:P, j, :].bitcast(F32), 0.0), begin, cleared,
                            mark=S("k_ones"))
                    kones = cleared = pool.do(lambda e, j=j: e.memset(
                        k_st[3 * HD:3 * HD + 2, j, :].bitcast(F32), 1.0), cleared,
                        mark=S("k_ones"))
                pool.need(kones)
                o_w = [[stage["qk"[k // 2]][p][:, k % 2 * D:(k % 2 + 1) * D] for k in range(KT)]
                       for p in range(2)]

                def v_jobs(free, toks):
                    return [split_job(piece, [q[:, k, :] for q in v_w], free, toks)
                            for k, piece in enumerate(wd["v"])]

                def v_weights(scope, n):
                    return [sbuf(scope, f"{tag}vw{n}{p}", [P, len(wd["v"]), D], F32R)
                            for p in range(2)]

                def piece_job(n, g, i):
                    at, w_in = (0, w_g[g][0]) if n == "q" else (2, w_g[g][1])
                    cols = slice(i * CH // 2, (i + 1) * CH // 2)
                    ps, ps_free = slots.take()
                    src = ps[:, 0, 0:CH // 2]
                    wv = [wmem[:, g % 2, at + p, :].rearrange("p (k m) -> p k m", k=KT)
                          for p in range(2)]
                    terms = [(wv[wp][:, k, :], hA[hp][:, k, cols]) for k in range(KT)
                             for wp, hp in THREE]
                    t = passes(src, terms, ps_free, w_in, hA_in[i // 2], mark=S("proj"))
                    w_free[g % 2][:] = [t]
                    hA_free[i // 2][:] = [t]
                    dst = [q[:, cols] for q in stage[n]]
                    yield
                    if not bias:
                        staged[n] += split_psum(src, dst, t, stage_free[n], ps_free, "qk",
                                                scale=scale if n == "q" else None)
                        return
                    _, buf, free = tmps.take()
                    col = bcol[:, g:g + 1] if n == "q" else bcol[:, 4:5]
                    r = dve.do(lambda e: e.scalar_tensor_tensor(
                        buf[:, 0:CH // 2], src, col, rope[n][:, cols], ALU.add, ALU.mult), t, free,
                        const_in, mark=S("rope"))
                    ps_free[:] = [r]
                    hi = act.do(lambda e: e.activation(dst[HI], buf[:, 0:CH // 2], ACT.Copy), r,
                                stage_free[n], mark=S("qk_hi"))
                    lo = dve.do(lambda e: e.tensor_tensor(dst[LO], buf[:, 0:CH // 2],
                                                          dst[HI].bitcast(F32), ALU.subtract),
                                hi, stage_free[n], mark=S("qk_lo"))
                    free[:] = [lo]
                    staged[n] += [hi, lo]

                def group_jobs(g):
                    names = "qk" if g == 0 or not grouped else "q"
                    for n in names:
                        staged[n] = []
                    return [piece_job(n, g, i) for n in names for i in range(4)]

                def group_weights(g):
                    w_g[g] = [[], []]
                    names = "qk" if g == 0 or not grouped else "q"
                    return [split_job(wd[n][g], [wmem[:, g % 2, 2 * i + p, :] for p in range(2)],
                                      w_free[g % 2], w_g[g][i]) for i, n in enumerate(names)]

                def stack(n, j, ready):
                    st, free = (q_st, q_free) if n == "q" else (k_st, k_free)
                    order = (HI, LO, HI) if n == "q" else (HI, HI, LO)
                    for r, part in enumerate(order):
                        t = sp.dma(st[r * HD:(r + 1) * HD, j, :].bitcast(F32),
                                   stage[n][part][j * HD:(j + 1) * HD, :].bitcast(F32),
                                   ready, free[j], kones, mark=S(f"{n}_st{j}"))
                    if n == "q":
                        t = sp.dma(st[3 * HD:3 * HD + 2, j, :].bitcast(F32), 
                                   k_st[P - 2:P, j, :].bitcast(F32), free[j],
                                   mark=S(f"{n}_st{j}"))
                    return t

                def v_split(tiles, src, ready, src_free):
                    tdims = dict(h=kv_heads, d=HD)
                    parts = [v[:, tiles, :, 1 + i * HD:1 + (i + 1) * HD] for i in range(3)]
                    s = src.rearrange("p (t h d) -> p t h d", **tdims)
                    v1 = act.do(lambda e: e.activation(parts[0], s, ACT.Copy), ready, v_free,
                                mark=S("v1"))
                    _, buf, free = tmps.take()
                    r = buf[:].rearrange("p (t h d) -> p t h d", **tdims)
                    r1 = dve.do(lambda e: e.tensor_tensor(r, s, parts[0], ALU.subtract), v1, free,
                                mark=S("v_rest"))
                    src_free[:] = [r1]
                    yield
                    v2 = act.do(lambda e: e.activation(parts[1], r, ACT.Copy), r1, v_free,
                                mark=S("v2"))
                    v3 = dve.do(lambda e: e.tensor_tensor(parts[2], r, parts[1], ALU.subtract), v2,
                                v_free, mark=S("v3"))
                    free[:] = [v3]
                    v_in.extend([v1, v2, v3])

                def v_tile_job(t):
                    ps, ps_free = slots.take()
                    terms = [(hA[hp][:, k, t * P:(t + 1) * P], v_w[wp][:, k, :])
                             for k in range(KT) for wp, hp in THREE]
                    tok = passes(ps[:, 0, :], terms, ps_free, v_w_in, hA_in[t // CT],
                                 mark=S("v_mm"))
                    hA_free[t // CT][:] = [tok]
                    v_last[0] = tok
                    yield from v_split(slice(t, t + 1), ps[:, 0, :], tok, ps_free)

                def v_chunk_job(c):
                    ps, ps_free = slots.take()
                    wv = [q[:, 0, :].rearrange("p (k m) -> p k m", k=KT) for q in v_w]
                    terms = [(wv[wp][:, k, :], hA[hp][:, k, c * CH:(c + 1) * CH])
                             for k in range(KT) for wp, hp in THREE]
                    t = passes(ps[:, 0, :], terms, ps_free, v_w_in, hA_in[c], mark=S("v_mm"))
                    v_last[0] = t
                    _, buf, free = tmps.take()
                    vb = act.do(lambda e: e.activation(buf[:], ps[:, 0, :], ACT.Identity,
                                                       bias=bcol[:, 5:6]), t, free, const_in,
                                mark=S("v_bias"))
                    ps_free[:] = [vb]
                    yield
                    ps2, ps2_free = slots.take()
                    pe.need(vb, ps2_free)
                    for i in range(CT):
                        tp = pe.do(lambda e, i=i: e.transpose(
                            ps2[:, 0, i * P:(i + 1) * P], buf[:, i * P:(i + 1) * P], ident[:]),
                            mark=S("v_tp"))
                    free[:] = [tp]
                    yield
                    yield from v_split(slice(c * CT, (c + 1) * CT), ps2[:, 0, :], tp, ps2_free)

                v_free = []
                v_last = [None]
                w_g = {g: [wmem_in[g][0], wmem_in[g][1]] for g in range(2)}
                e_jobs = Jobs()
                v_w_in = []
                v_scope = sc.enter_context(ExitStack())
                v_w = v_weights(v_scope, 0)
                e_jobs.waiting += v_jobs(begin, v_w_in)
                for b in range(BATCH):
                    staged, v_in = {}, []
                    if bias:
                        for t in range(b * ST, (b + 1) * ST):
                            x_ready[t] = pool.do(lambda e, t=t: e.tensor_tensor(
                                x[:, t, :], x[:, t, :], bo[:], ALU.add), S_last["rstd"],
                                x_ready[t], const_in, mark=S("x_pool"))
                    first = Jobs()
                    first.waiting += group_jobs(0)
                    while first.waiting or first.running:
                        first.tick()
                        e_jobs.tick()
                    e_jobs.flush()
                    q_in = [None] * HPG
                    if not grouped or b == 0:
                        k_in = [None] * HPG

                    def stack_head(n, j):
                        token = stack(n, j, list(staged[n]))
                        (q_in if n == "q" else k_in)[j] = token
                        stage_free[n][:] = stage_free[n][-(HPG - 1):] + [token]

                    for j in range(HPG):
                        for n in "qk":
                            stack_head(n, j)

                    def halves(ps, width):
                        return ps[:, 0:1, 0:width] if width <= CH else ps[:, :, 0:width // 2]

                    def head_of(n):
                        g, j = n // HPG, n % HPG
                        return (HPG * j + g, j, j) if grouped else (n, j, n)

                    def row_max(n, i):
                        _, j, _ = head_of(n)
                        w_ = (i + 1) * P
                        cols = max(w_, 2 * P)
                        pieces = 1 if cols <= CH else 2
                        ps, ps_free = slots.take(pieces)
                        pe.need(ps_free, q_in[j], k_in[j], consts)
                        pw = cols // pieces
                        for z in range(pieces):
                            pe.do(mm(ps[:, z, 0:pw], q_st[:, j, i * P:(i + 1) * P],
                                     k_st[:, j, z * pw:(z + 1) * pw], True, True))
                        end = w_ - (pieces - 1) * pw
                        t = pe.do(mm(ps[:, pieces - 1, end - P:end], ident_b[:], mask_q[:], False,
                                     True, True), mark=S("s_q"))
                        mx = dve.do(lambda e: e.tensor_reduce(
                            negmax[:, i:i + 1], halves(ps, w_), AX.XY, ALU.max, negate=True), t,
                            S_last.get("negmax"), mark=S("row_max"))
                        ps_free[:] = [mx]
                        return mx

                    def max_job(n, mx):
                        _, j, _ = head_of(n)
                        _, mc, mc_free = mcol.take()
                        hi = dve.do(lambda e: e.tensor_copy(mc[:, 0:ST].bitcast(F32R), negmax[:]),
                                    mx, mc_free, mark=S("m_split"))
                        lo = dve.do(lambda e: e.tensor_tensor(mc[:, ST:2 * ST], negmax[:],
                                                              mc[:, 0:ST], ALU.subtract), hi,
                                    mark=S("m_split"))
                        S_last["negmax"] = lo
                        yield
                        ps, ps_free = slots.take()
                        tp = pe.do(lambda e: e.transpose(ps[0:2 * ST, 0, 0:P], mc[:], ident[:]),
                                   lo, ps_free, mark=S("m_tp"))
                        mc_free[:] = [tp]
                        i, mr, mr_free = mrow.take()
                        cp = act.do(lambda e: e.activation(mr[:], ps[0:2 * ST, 0, 0:P], ACT.Copy),
                                    tp, mr_free, mark=S("m_row"))
                        ps_free[:] = [cp]
                        for r in range(2):
                            row = q_st[3 * HD + r:3 * HD + r + 1, j, :].bitcast(F32)
                            t = sp.dma(row.rearrange("o (i q) -> o i q", q=P),
                                       mr[r * ST:(r + 1) * ST, :], cp, q_free[j],
                                       mark=S(f"m_in{n % 2}"))
                        mr_free[:] = [t]
                        m_in[n] = t

                    def exp_keys(n, jt, m_in):
                        head, j, kv = head_of(n)
                        w_ = SEQ - jt * P
                        cols = max(w_, 2 * P)
                        pieces = 1 if cols <= CH else 2
                        pw, q0 = cols // pieces, SEQ - cols
                        skip = cols - w_
                        ps, ps_free = slots.take(pieces)
                        pe.need(ps_free, m_in, kones)
                        for z in range(pieces):
                            pe.do(mm(ps[:, z, 0:pw], k_st[:, j, jt * P:(jt + 1) * P],
                                     q_st[:, j, q0 + z * pw:q0 + (z + 1) * pw],
                                     True, True))
                        t = pe.do(mm(ps[:, 0, skip:skip + P], ident_b[:], mask_k[:], False, True,
                                     True), mark=S("s_k"))
                        if jt == ST - 1:
                            q_free[j][:] = [t]
                            if not grouped or n // HPG == HPG - 1:
                                k_free[j][:] = [t]
                        _, e_, e_free = e32.take()
                        src = halves(ps, w_) if pieces == 2 else ps[:, 0:1, skip:skip + w_]
                        dst = e_[:, 0:w_].rearrange("p (z w) -> p z w", z=pieces)
                        ex = act.do(lambda e: e.activation(dst, src, ACT.Exp, bias=p_scale[:]),
                                    t, e_free, consts, mark=S("exp"))
                        ps_free[:] = [ex]
                        _, (eh, el), e16_free = e16.take()
                        hi = None
                        if jt in HI_ON_ACT:
                            hi = act.do(lambda e: e.activation(
                                eh[:, 0:w_].rearrange("p (z w) -> p z w", z=pieces), src, ACT.Exp,
                                bias=p_scale[:]), e16_free, mark=S("p_hi_act"))
                            ps_free[:] = [hi]
                        return n, jt, w_, e_, e_free, ex, eh, el, e16_free, hi

                    def split_exp(n, jt, w_, e_, e_free, ex, eh, el, e16_free, hi):
                        if hi is None:
                            hi = dve.do(lambda e: e.tensor_copy(eh[:, 0:w_], e_[:, 0:w_]), ex,
                                        e16_free, mark=S("p_hi_dve"))
                        lane, nm = (pool, "p_lo_pool") if jt in LO_ON_POOL else (dve, "p_lo_dve")
                        lo = lane.do(lambda e: e.tensor_tensor(el[:, 0:w_], e_[:, 0:w_],
                                                               eh[:, 0:w_], ALU.subtract), hi,
                                     e16_free, mark=S(nm))
                        e_free[:] = [lo]
                        return n, jt, eh, el, [hi, lo], e16_free

                    acc_free = banks.free

                    def times_v(n, jt, eh, el, ready, e16_free):
                        head, _, kv = head_of(n)
                        pe.need(ready, v_in, ones)
                        if jt == 0:
                            pe.need(acc_free[0], acc_free[1])
                        for i in range(jt, ST):
                            o = acc[:, i // CT, i % CT * VW:i % CT * VW + 1 + 3 * HD]
                            q = slice((i - jt) * P, (i - jt + 1) * P)
                            first = jt == 0 and i % CT == 0
                            pe.do(mm(o, eh[:, q], v[:, jt, kv, 0:1 + 3 * HD], first, False, True))
                            t = pe.do(mm(o[:, 0:1 + 2 * HD], el[:, q], v[:, jt, kv, 0:1 + 2 * HD],
                                         False, i == jt, True),
                                      mark=S("pv") if i in (CT - 1, ST - 1) or i == jt else None)
                            if i == jt and i in (CT - 1, ST - 1):
                                take_y(n, i // CT, t)
                        e16_free[:] = [t]

                    def take_y(n, bank, t):
                        head, _, _ = head_of(n)
                        o = acc[:, bank, 0:CT * VW].rearrange("p (i w) -> p i w", w=VW)
                        parts = o[:, :, 1:1 + 3 * HD].rearrange("p i (s d) -> p i d s", s=3)
                        i0 = bank * CT
                        dve.do(lambda e: e.tensor_reduce(
                            y[:, i0:i0 + CT, head * HD:(head + 1) * HD], parts, AX.X, ALU.add), t,
                            y_free, mark=S("y_take"))
                        r = dve.do(lambda e: e.tensor_copy(den[:, i0:i0 + CT, head:head + 1],
                                                           o[:, :, 0:1]), t, y_free,
                                   mark=S("y_take"))
                        acc_free[bank][:] = [r]
                        taken[0] = r

                    taken = [None]
                    m_in = {}

                    def row_unit(u):
                        n, i = divmod(u, ST)
                        if n < HEADS:
                            mx = row_max(n, (u - AHEAD) % ST)
                            if i == ST - 1:
                                side.start(max_job(n, mx))

                    side = Jobs()
                    if grouped:
                        side.waiting += [v_chunk_job(c) for c in range(2)]
                    else:
                        side.waiting += [v_tile_job(t) for t in range(ST)]
                    tiles = len(side.waiting)
                    for u in range(AHEAD):
                        side.tick(start=(u * tiles) // AHEAD != ((u - 1) * tiles) // AHEAD)
                        row_unit(u)
                    side.flush()
                    v_scope.close()
                    heads_scope = sc.enter_context(ExitStack())
                    e32 = Ring([sbuf(heads_scope, f"{tag}e{b}{i}", [P, SEQ]) for i in range(3)],
                               [v_last[0]])
                    e16 = Ring([[sbuf(heads_scope, f"{tag}e{b}{p}{i}", [P, SEQ], F16)
                                 for p in range(2)] for i in range(4)], [v_last[0]])

                    GU = HPG * ST
                    beside = {}
                    o_in = []
                    last = (HPG - 1) * GU
                    fresh, behind = [], []
                    for u in range(HEADS * ST):
                        n, i = divmod(u, ST)
                        g, at = divmod(u, GU)
                        if at == 0 and g + 1 < HPG:
                            beside.update({u + 2 * k: job for k, job in
                                           enumerate(group_jobs(g + 1))})
                        if at == 20 and g + 2 < HPG:
                            beside.update({u + 2 * k: job for k, job in
                                           enumerate(group_weights(g + 2))})
                        if u == last + 2:
                            jobs = [split_job(wd["o"][k], [o_w[p][k] for p in range(2)],
                                              [stage_free["q"], stage_free["k"]], o_in)
                                    for k in range(KT)]
                            w_all = [w_free[0][:], w_free[1][:]]
                            if b + 1 < BATCH:
                                jobs += group_weights(0) + group_weights(1)
                            elif then:
                                jobs += then(w_all, buffers)
                            step = (GU - 4) // len(jobs)
                            beside.update({u + step * k: job for k, job in enumerate(jobs)})
                        row_unit(u + AHEAD)
                        fresh.append(exp_keys(n, i, m_in[n]))
                        if len(fresh) > 1:
                            behind.append(split_exp(*fresh.pop(0)))
                        if len(behind) > 2:
                            times_v(*behind.pop(0))
                        side.tick()
                        if u in beside:
                            side.start(beside.pop(u))
                        if g + 1 < HPG:
                            for j, when in enumerate((17, 18, 24, 31)):
                                if at == when:
                                    for m in "qk" if not grouped else "q":
                                        stack_head(m, j)
                    side.flush()
                    behind.append(split_exp(*fresh.pop()))
                    for unit in behind:
                        times_v(*unit)
                    v_free[:] = [pe.last]

                    now = ends()
                    heads_scope.close()
                    if b + 1 < BATCH:
                        v_w_in = []
                        v_scope = sc.enter_context(ExitStack())
                        v_w = v_weights(v_scope, b + 1)
                        e_jobs.waiting += v_jobs(now, v_w_in)
                    proj_scope = sc.enter_context(ExitStack())
                    yT = Ring([[sbuf(proj_scope, f"{tag}yT{b}{i}{p}", [P, KT, P], F32R)
                                for p in range(2)] for i in range(2)], now)
                    if b + 1 < BATCH or then:
                        for half in range(2):
                            hA_norm(half + 2 if b + 1 < BATCH else half, half)
                    rec = dve.do(lambda e: e.reciprocal(den[:], den[:]), taken[0], mark=S("recip"))

                    def turn(t):
                        yn = pool.do(lambda e: e.tensor_tensor(
                            y[:, t, :].rearrange("p (h d) -> p h d", d=HD),
                            y[:, t, :].rearrange("p (h d) -> p h d", d=HD),
                            den[:, t, :].unsqueeze(2).to_broadcast([P, HEADS, HD]), ALU.mult), rec,
                            mark=S("y_norm"))
                        ps, ps_free = slots.take()
                        pe.need(yn, ps_free)
                        for k in range(KT):
                            tp = pe.do(lambda e, k=k: e.transpose(
                                ps[:, 0, k * P:(k + 1) * P], y[:, t, k * P:(k + 1) * P], ident[:]),
                                mark=S("y_tp") if k == KT - 1 else None)
                        src = ps[:, 0, :].rearrange("p (k q) -> p k q", k=KT)
                        _, yt, yT_free = yT.take()
                        toks = split_psum(src, [q[:] for q in yt], tp, yT_free, ps_free, "y")
                        y_free[:] = [tp]
                        return yt, toks, yT_free

                    def project_out(t, yt, toks, yT_free):
                        i, bank, free = banks.take()
                        terms = [(yt[yp][:, k, :], o_w[wp][k]) for k in range(KT)
                                 for wp, yp in THREE]
                        o = passes(bank, terms, free, toks, o_in, mark=S("o_proj"))
                        yT_free[:] = [o]
                        tt = b * ST + t
                        x_ready[tt] = dve.do(lambda e: e.tensor_tensor(
                            x[:, tt, :], bank, x[:, tt, :], ALU.add), o, x_ready[tt],
                            S_last["rstd"], mark=S("x_add"))
                        free[:] = [x_ready[tt]]
                        for n in "qk":
                            stage_free[n][:] = [o]

                    turned = turn(0)
                    for t in range(ST):
                        now_, turned = turned, turn(t + 1) if t + 1 < ST else None
                        norms.tick()
                        e_jobs.tick()
                        project_out(t, *now_)
                    norms.flush()
                    proj_scope.close()

        AHEAD = 13
        HI_ON_ACT = (1, 3, 6)
        LO_ON_POOL = (0, 2, 4, 5, 7)

        ffn0 = ("f0", a["gate0"], a["up0"], a["down0"], 1536, 384,
                (a["gscale"], a["uscale"], a["dscale"].partition_broadcast(P)), True)
        ffn1 = ("f1", a["gate1"], a["up1"], a["down1"], 2048, 256, None, False)
        score_scale = float(1.0 / np.sqrt(np.float32(HD)))
        w0 = {n: [a[n + "0"][i] for i in range(k)] for n, k in
              (("q", 4), ("k", 1), ("v", 1), ("o", 4))}
        w1 = {n: [a[n + "1"][i] for i in range(4)] for n in "qkvo"}
        def first_weights(stage):
            if stage == "f0":
                return (lambda free, buffers: ffn_first_weights(*ffn0[1:3], True, free, buffers)), True
            if stage == "f1":
                return (lambda free, buffers: ffn_first_weights(*ffn1[1:3], False, free, None)), False
            return (lambda free, buffers: attention_first_weights(
                w0 if stage == "a0" else w1, free)), False

        def attention_first_weights(wd, free):
            toks, jobs = [[[], []], [[], []]], []
            for g in range(2):
                for i, n in enumerate("qk"):
                    if g < len(wd[n]):
                        jobs.append(split_job(wd[n][g], [wmem[:, g, 2 * i + p, :]
                                                         for p in range(2)], free, toks[g][i]))
            wmem_in[:] = toks
            return jobs

        with ExitStack() as sc:
            load, fp8 = first_weights(STAGES[0])
            hA_norm(0, 0)
            hA_norm(1, 1)
            weights.waiting += load([], fp8_buffers(sc, "first", 3) if fp8 else None)
            while norms.waiting or norms.running or weights.waiting or weights.running:
                tick()

        for n, s in enumerate(STAGES):
            then, fp8 = first_weights(STAGES[n + 1]) if n + 1 < len(STAGES) else (None, False)
            if s == "f0":
                ffn(f"s{n}" + ffn0[0], *ffn0[1:], then)
            elif s == "f1":
                ffn(f"s{n}" + ffn1[0], *ffn1[1:], then)
            elif s == "a0":
                attention("a0", w0, KV0, score_scale,
                          (a["rope"], a["bq"], a["bk"], a["bv"], a["bo"].partition_broadcast(P)),
                          then, fp8)
            else:
                attention("a1", w1, HEADS, score_scale, None, then, fp8)

        out_rows = out.rearrange("(t p) d -> t p d", p=P)
        for t in range(NT):
            done = sp.dma(out_rows[t], x[:, t, :], x_ready[t], mark=S("out"))
        sp.need(done)

        with nc.Block() as block:
            block.sync(sp.play)
            block.tensor(pe.play)
            block.scalar(act.play)
            block.vector(dve.play)
            block.gpsimd(pool.play)


STAGES = ("f0", "a0", "f0", "f1", "a1", "f1")


def rope_table():
    inv = np.float32(10000.0) ** (np.float32(-2.0) * np.arange(HD // 2, dtype=np.float32)
                                  / np.float32(HD))
    theta = np.arange(SEQ, dtype=np.float32)[:, None] * inv[None, :]
    table = np.tile((np.cos(theta) + np.sin(theta)).T, (2 * HPG, 1)).astype(np.float32)
    return np.stack([table / np.sqrt(np.float32(HD)), table]).astype(np.float32)


def layouts(i):
    def gate(w, gw):
        n = w.shape[1] // gw
        return w.reshape(KT, P, n, gw).transpose(2, 1, 0, 3).reshape(n, P, KT * gw)

    def down(w, gw):
        n = w.shape[0] // gw
        return w.reshape(n, gw // P, P, D).transpose(0, 2, 1, 3).reshape(n, P, gw // P * D)

    def cols(w):
        n = w.shape[1] // P
        return w.reshape(KT, P, n, P).transpose(2, 1, 0, 3).reshape(n, P, KT * P)

    def rows(w):
        return w.reshape(KT, P, D)

    def regroup(w):
        return w.reshape(*w.shape[:-1], HPG, HPG, HD).swapaxes(-3, -2).reshape(w.shape)

    wa = i["L1_attn_w_attn"]
    return {
        "x": i["L0_attn_x"].reshape(TOK, D),
        "gate0": gate(i["L0_ffn_gate_w"], 384), "up0": gate(i["L0_ffn_up_w"], 384),
        "down0": down(i["L0_ffn_down_w"], 384),
        "gscale": i["L0_ffn_gate_scale"].reshape(-1, P).T,
        "uscale": i["L0_ffn_up_scale"].reshape(-1, P).T,
        "dscale": i["L0_ffn_down_scale"],
        "gate1": gate(i["L1_ffn_w_gate"].T, 256), "up1": gate(i["L1_ffn_w_up"].T, 256),
        "down1": down(i["L1_ffn_w_down"].T, 256),
        "q0": cols(regroup(i["L0_attn_Wq"].T)), "k0": cols(i["L0_attn_Wk"].T),
        "v0": cols(i["L0_attn_Wv"].T), "o0": rows(i["L0_attn_Wo"].T),
        "bq": regroup(i["L0_attn_bq"]).reshape(HPG, P).T, "bk": i["L0_attn_bk"].reshape(P, 1),
        "bv": i["L0_attn_bv"].reshape(P, 1), "bo": i["L0_attn_bo"],
        "q1": cols(wa[:, 0:D]), "k1": cols(wa[:, D:2 * D]), "v1": rows(wa[:, 2 * D:3 * D]),
        "o1": rows(i["L1_attn_w_proj"]),
        "rope": rope_table(),
    }


def kernel(**inputs):
    import concourse.bacc as bacc
    from concourse.bass_utils import run_bass_kernel_spmd

    arrays = {f"in_{n}": np.ascontiguousarray(v) for n, v in
              layouts({n: np.asarray(v) for n, v in inputs.items()}).items()}
    nc = bacc.Bacc("TRN2", target_bir_lowering=False, num_devices=1)
    aps = {n[3:]: nc.dram_tensor(n, v.shape, F32, kind="ExternalInput").ap() for n, v in arrays.items()}
    out = nc.dram_tensor("out", (TOK, D), F32, kind="ExternalOutput").ap()
    build(nc, aps, out)
    r = run_bass_kernel_spmd(nc, [arrays], core_ids=[0])
    return r.results[0]["out"].reshape(BATCH, SEQ, D)
```

```python
from contextlib import ExitStack

import numpy as np

import concourse.bass as bass
from concourse import mybir

F32 = mybir.dt.float32
F32R = mybir.dt.float32r
F16 = mybir.dt.float16
BF16 = mybir.dt.bfloat16
FP8 = mybir.dt.float8e4
ALU = mybir.AluOpType
ACT = mybir.ActivationFunctionType
AX = mybir.AxisListType

P = 128
BATCH, SEQ, D = 2, 1024, 512
TOK = BATCH * SEQ
NT = TOK // P
ST = SEQ // P
KT = D // P
CH = 512
NC = TOK // CH
CT = CH // P
HEADS, HD = 16, 32
HPG = P // HD
KV0 = 4
VW = 98
EPS = 1e-5
MASKED = -1e30
FP8_TRN_MAX = 240.0
FP8_FN_MAX = 448.0
NAN_SCALE = 3.4e38 / 464.0
P_SCALE_LN = float(np.log(1024.0))


class Lane:

    def __init__(self, name):
        self.name, self.ops, self.seen, self.last = name, [], {}, None

    def need(self, *tokens):
        for t in tokens:
            if isinstance(t, list):
                self.need(*t)
            elif t is not None and self.seen.get(t[0].name, 0) < t[1]:
                self.seen[t[0].name] = t[1]
                self.ops.append((None, t[0].handle, t[1]))

    def do(self, emit, *tokens, mark=None):
        self.need(*tokens)
        token = mark.up(1) if mark else None
        self.ops.append((emit, mark.handle if mark else None, 1))
        self.last = token
        return token

    def dma(self, out, in_, *tokens, mark):
        self.need(*tokens)
        token = mark.up(16)
        self.ops.append((lambda e, out=out, in_=in_: e.dma_start(out, in_), mark.handle, 16))
        return token

    def play(self, engine):
        for emit, sem, value in self.ops:
            if emit is None:
                engine.wait_ge(sem, value)
            else:
                ins = emit(engine)
                if sem is not None:
                    ins.then_inc(sem, value)


class Sem:
    def __init__(self, ctx, nc, name):
        self.name, self.handle, self.count = name, ctx.enter_context(nc.semaphore(name)), 0

    def up(self, by):
        self.count += by
        return self, self.count


class Readers(list):

    def __init__(self, tokens=()):
        super().__init__(tokens)
        self.in_use = False

    def __setitem__(self, key, tokens):
        super().__setitem__(key, tokens)
        self.in_use = False

    def hand_out(self):
        assert not self.in_use
        self.in_use = True
        return self


class Ring:

    def __init__(self, views, free=()):
        self.views, self.free, self.at = views, [Readers(free) for _ in views], 0

    def take(self):
        i = self.at % len(self.views)
        self.at += 1
        return i, self.views[i], self.free[i].hand_out()


class Strip:

    def __init__(self, views, free=()):
        self.views, self.size, self.at = views, views[0].shape[1], 0
        self.held = [(0, self.size, Readers(free))]

    def take(self, width):
        begin = self.at if self.at + width <= self.size else 0
        end = self.at = begin + width
        before, kept = [], []
        for b, e, readers in self.held:
            if b < end and e > begin:
                assert not readers.in_use
                before += readers
                kept += [(x, y, readers) for x, y in ((b, begin), (end, e)) if x < y]
            else:
                kept.append((b, e, readers))
        readers = Readers(before)
        self.held = kept + [(begin, end, readers)]
        return [v[:, begin:end] for v in self.views], readers.hand_out()


class Banks:

    def __init__(self, view):
        self.view = view
        self.free = [Readers() for _ in range(view.shape[1])]
        self.order = list(range(view.shape[1]))

    def take(self, width=1):
        age = {bank: n for n, bank in enumerate(self.order)}
        spans = [range(i, i + width) for i in range(len(self.free) - width + 1)
                 if not any(f.in_use for f in self.free[i:i + width])]
        banks = min(spans, key=lambda span: max(age[i] for i in span))
        free = Readers([t for i in banks for t in self.free[i]])
        for i in banks:
            self.free[i] = free
            self.order.remove(i)
            self.order.append(i)
        return self.view[:, banks[0]:banks[-1] + 1, :], free.hand_out()


class Jobs:

    def __init__(self):
        self.waiting, self.running = [], []
        self.every, self.ticks = 1, 0

    def tick(self, start=True):
        self.running = [job for job in self.running if next(job, "done") != "done"]
        self.ticks += 1
        if start and self.waiting and self.ticks % self.every == 0:
            self.start(self.waiting.pop(0))

    def start(self, job):
        if next(job, "done") != "done":
            self.running.append(job)

    def finish(self, job):
        while job in self.waiting or job in self.running:
            self.tick()

    def flush(self):
        while self.waiting or self.running:
            self.tick()


def build(nc, a, out):
    with ExitStack() as ctx:
        pe, act, dve, pool, sp = (Lane(n) for n in ("pe", "act", "dve", "pool", "sp"))
        sems = {}

        def S(name):
            if name not in sems:
                sems[name] = Sem(ctx, nc, name)
            return sems[name]

        def sbuf(scope, name, shape, dt=F32):
            return scope.enter_context(nc.sbuf_tensor(name, shape, dt))

        x = sbuf(ctx, "x", [P, NT, D])
        hA = [sbuf(ctx, f"hA_{p}", [P, KT, SEQ], F32R) for p in ("hi", "lo")]
        ident = sbuf(ctx, "ident", [P, P])
        ident_b = sbuf(ctx, "ident_b", [P, P], BF16)
        mask_q = sbuf(ctx, "mask_q", [P, P], BF16)
        mask_k = sbuf(ctx, "mask_k", [P, P], BF16)
        stats = sbuf(ctx, "stats", [P, CT, 6])
        meanvar = sbuf(ctx, "meanvar", [P, NT, 2])
        rstd = sbuf(ctx, "rstd", [P, NT])
        minus_half = sbuf(ctx, "minus_half", [P, CT])
        p_scale = sbuf(ctx, "p_scale", [P, 1])
        tmp = [sbuf(ctx, f"tmp{i}", [P, D]) for i in range(2)]
        raw = Ring([sbuf(ctx, f"raw{i}", [P, D]) for i in range(2)])
        wmem = sbuf(ctx, "wmem", [P, 2, 4, D], F32R)

        psum = ctx.enter_context(nc.psum_tensor("psum", [P, 6, 512], F32))
        acc = ctx.enter_context(nc.psum_tensor("acc", [P, 2, 512], F32))
        slots = Banks(psum[:, :, :])
        banks = Ring([acc[:, 0, :], acc[:, 1, :]])
        tmps = Ring(tmp)

        c0 = pool.do(lambda e: e.memset(ident[:], 0.0), mark=S("const"))
        c1 = pool.do(lambda e: e.memset(ident_b[:], 0.0), mark=S("const"))
        c2 = pool.do(lambda e: e.memset(mask_q[:], 0.0), mark=S("const"))
        c3 = pool.do(lambda e: e.memset(mask_k[:], 0.0), mark=S("const"))
        pool.do(lambda e: e.memset(minus_half[:], -0.5), mark=S("const"))
        pool.do(lambda e: e.memset(p_scale[:], P_SCALE_LN), mark=S("const"))
        for t in (ident, ident_b):
            pool.do(lambda e, t=t: e.affine_select(
                out=t[:], in_=t[:], compare_op=ALU.not_equal, fill=1.0, base=0,
                pattern=[[-1, P]], channel_multiplier=1), c0, c1, c2, c3, mark=S("const"))
        pool.do(lambda e: e.affine_select(
            out=mask_q[:], in_=mask_q[:], compare_op=ALU.is_ge, fill=MASKED, base=0,
            pattern=[[-1, P]], channel_multiplier=1), mark=S("const"))
        consts = pool.do(lambda e: e.affine_select(
            out=mask_k[:], in_=mask_k[:], compare_op=ALU.is_ge, fill=MASKED, base=0,
            pattern=[[1, P]], channel_multiplier=-1), mark=S("const"))

        x_rows = a["x"].rearrange("(t p) d -> t p d", p=P)
        x_ready = [sp.dma(x[:, t, :], x_rows[t], mark=S(f"x_in{t}")) for t in range(CT)]
        x_read = [None] * NT

        def mm(out_, lhsT, rhs, start, stop, skip=False):
            return lambda e: e.matmul(out_, lhsT, rhs, start=start, stop=stop,
                                      skip_group_check=skip)

        def passes(out_, terms, *tokens, mark=None):
            pe.need(*tokens)
            for n, (w, m) in enumerate(terms):
                last = n == len(terms) - 1
                t = pe.do(mm(out_, w, m, n == 0, last), mark=mark if last else None)
            return t

        HI, LO = 0, 1
        THREE = ((HI, HI), (HI, LO), (LO, HI))

        def norm_stats(t):
            st = dve.do(lambda e: e.bn_stats(stats[:, t % CT, :], x[:, t, :]),
                        x_ready[t], S_last.get("stats"), mark=S("ln_stats"))
            S_last["stats"] = ag = dve.do(
                lambda e: e.bn_aggr(meanvar[:, t, :], stats[:, t % CT, :]), st, mark=S("ln_stats"))
            ve = pool.do(lambda e: e.tensor_scalar(rstd[:, t:t + 1], meanvar[:, t, 1:2], EPS, None,
                                                   ALU.add), ag, S_last.get("rstd"), mark=S("ln_rstd"))
            return pool.do(lambda e: e.tensor_tensor(rstd[:, t:t + 1], rstd[:, t:t + 1],
                                                     minus_half[:, 0:1], ALU.pow), ve, consts,
                           mark=S("ln_rstd"))

        S_last = {}


        def norm_jobs(c, h, h_free, toks):
            def tile_job(i):
                t, at = c * CT + i, i * P
                rs = norm_stats(t)
                yield
                _, buf, free = tmps.take()
                hn = dve.do(lambda e: e.tensor_scalar(buf[:], x[:, t, :], meanvar[:, t, 0:1],
                                                      rstd[:, t:t + 1], ALU.subtract, ALU.mult),
                            rs, free, mark=S("ln_out"))
                S_last["rstd"] = hn
                yield
                ps, ps_free = slots.take()
                pe.need(hn, ps_free, consts)
                for k in range(KT):
                    tp = pe.do(lambda e, k=k: e.transpose(ps[:, 0, k * P:(k + 1) * P],
                                                          buf[:, k * P:(k + 1) * P], ident[:]),
                               mark=S("ln_tp") if k == KT - 1 else None)
                free[:] = [tp]
                src = ps[:, 0, :].rearrange("p (k q) -> p k q", k=KT)
                dst = [q[:, :, at:at + P] for q in h]
                hi = act.do(lambda e: e.activation(dst[HI], src, ACT.Copy), tp, h_free,
                            mark=S("ln_hi"))
                yield
                lo = dve.do(lambda e: e.tensor_tensor(dst[LO], src, dst[HI].bitcast(F32),
                                                      ALU.subtract), hi, h_free, mark=S("ln_lo"))
                ps_free[:] = [lo]
                toks.extend([hi, lo])
            return [tile_job(i) for i in range(CT)]

        def split_job(src, dst, free, toks):
            i, rb, r_free = raw.take()
            landed = sp.dma(rb[:], src, r_free, mark=S(f"raw{i}"))
            yield
            hi = act.do(lambda e: e.activation(dst[HI], rb[:], ACT.Copy), landed, free,
                        mark=S("w_hi"))
            lo = pool.do(lambda e: e.tensor_tensor(dst[LO], rb[:], dst[HI].bitcast(F32),
                                                   ALU.subtract), hi, free, mark=S("w_lo"))
            r_free[:] = [lo]
            toks.extend([hi, lo])

        def fp8_buffers(scope, tag, n):
            return Ring([([sbuf(scope, f"{tag}q8{i}{k}", [P, D], FP8) for k in range(2)],
                          [sbuf(scope, f"{tag}qb{i}{k}", [P, D], BF16) for k in range(3)],
                          sbuf(scope, f"{tag}qz{i}", [P, D])) for i in range(n)], ends())

        def round_job(src, dst, free, toks, buffers):
            i, rb, r_free = raw.take()
            landed = sp.dma(rb[:], src, r_free, mark=S(f"raw{i}"))
            yield
            _, (q8, qb, qz), q_free = buffers.take()
            one = act.do(lambda e: e.activation(q8[0][:], rb[:], ACT.Copy, saturate=False),
                         landed, q_free, mark=S("q8"))
            half = act.do(lambda e: e.activation(q8[1][:], rb[:], ACT.Copy, scale=0.5,
                                                 saturate=False), mark=S("q8"))
            r_free[:] = [half]
            yield
            m = FP8_TRN_MAX
            low = dve.do(lambda e: e.tensor_scalar(qb[0][:], q8[0][:], m, -m, ALU.min,
                                                   ALU.max), one, q_free, mark=S("q_dve"))
            clp = dve.do(lambda e: e.tensor_scalar(qb[1][:], q8[1][:], m / 2, -m / 2,
                                                   ALU.min, ALU.max), half, mark=S("q_dve"))
            over = dve.do(lambda e: e.tensor_tensor(qb[2][:], q8[1][:], qb[1][:], ALU.subtract),
                          clp, q_free, mark=S("q_dve"))
            yield
            q = dve.do(lambda e: e.scalar_tensor_tensor(qb[0][:], qb[2][:], 2.0, qb[0][:],
                                                        ALU.mult, ALU.add), low, over,
                       mark=S("q_dve"))
            z = dve.do(lambda e: e.tensor_scalar(qz[:], qb[0][:], NAN_SCALE, 0.0, ALU.mult,
                                                 ALU.mult), q, q_free, mark=S("q_dve"))
            res = pool.do(lambda e: e.tensor_tensor(dst, qb[0][:], qz[:], ALU.add), z,
                          free, mark=S("q_pool"))
            q_free[:] = [res]
            toks.append(res)

        def split_psum(src, dst, ready, dst_free, src_free, tag, scale=None):
            hi = act.do(lambda e: e.activation(dst[HI], src, ACT.Copy,
                                               scale=1.0 if scale is None else scale),
                        ready, dst_free, mark=S(f"{tag}_hi"))
            hi32 = dst[HI].bitcast(F32)
            if scale is None:
                lo = dve.do(lambda e: e.tensor_tensor(dst[LO], src, hi32, ALU.subtract),
                            hi, dst_free, mark=S(f"{tag}_lo"))
            else:
                lo = dve.do(lambda e: e.scalar_tensor_tensor(dst[LO], src, scale, hi32, ALU.mult,
                                                             ALU.subtract),
                            hi, dst_free, mark=S(f"{tag}_lo"))
            src_free[:] = [lo]
            return [hi, lo]

        def ends():
            return [l.last for l in (pe, act, dve, pool) if l.last is not None]

        hA_free = [[] for _ in range(2)]
        hA_in = [[], []]
        wmem_in = []
        hA_jobs = [None, None]
        norms, weights = Jobs(), Jobs()

        def tick():
            norms.tick()
            weights.tick()

        def hA_norm(c, half):
            hA_in[half] = []
            h = [q[:, :, half * CH:(half + 1) * CH] for q in hA]
            jobs = norm_jobs(c, h, hA_free[half], hA_in[half])
            hA_jobs[half] = jobs[-1]
            norms.waiting += jobs

        def ffn_first_weights(gate_d, up_d, quantised, free, buffers):
            flat = wmem[:].rearrange("p a b d -> p (a b d)")
            jobs, at = [], 0
            wmem_in[:] = [[], []]
            for toks, src in zip(wmem_in, (gate_d, up_d)):
                pieces = src.shape[2] // D
                for i in range(pieces):
                    cols = src[0][:, i * D:(i + 1) * D]
                    if quantised:
                        jobs.append(round_job(cols, flat[:, at + i * D:at + (i + 1) * D], free,
                                              toks, buffers))
                    else:
                        lo = at + (pieces + i) * D
                        jobs.append(split_job(cols, [flat[:, at + i * D:at + (i + 1) * D],
                                                     flat[:, lo:lo + D]], free, toks))
                at += pieces * D * (1 if quantised else 2)
            return jobs

        def ffn(tag, gate_d, up_d, down_d, hidden, gw, scales, quantised, then):
            with ExitStack() as sc:
                begin = ends()
                groups, MT = hidden // gw, gw // P
                parts = 1 if quantised else 2
                hB = [sbuf(sc, f"{tag}hB{p}", [P, KT, SEQ], F32R) for p in range(2)]
                h = [[q[:, :, c % 2 * CH:(c % 2 + 1) * CH] for q in (hA, hB)[c // 2]]
                     for c in range(NC)]
                h_free = [hA_free[0], hA_free[1], list(begin), list(begin)]
                wn = KT * gw
                flat = wmem[:].rearrange("p a b d -> p (a b d)")
                w = [[[flat[:, (n * parts + p) * wn:(n * parts + p + 1) * wn] if b == 0 and n < 2
                       else sbuf(sc, f"{tag}w{n}{b}{p}", [P, wn], F32R)[:] for p in range(parts)]
                      for n in range(3)] for b in range(2)]
                w_free = [list(begin), list(begin)]
                act_ = [[sbuf(sc, f"{tag}a{b}{p}", [P, MT, CH], F32R) for p in range(2)]
                        for b in range(2)]
                a_free = [list(begin), list(begin)]
                silu = Ring([sbuf(sc, f"{tag}silu{i}", [P, CH]) for i in range(2)], begin)
                prod = Ring([sbuf(sc, f"{tag}prod{i}", [P, CH]) for i in range(2)], begin)
                buffers = fp8_buffers(sc, tag, 3) if quantised else None
                if quantised:
                    gs = sbuf(sc, f"{tag}gs", [P, hidden // P])
                    us = sbuf(sc, f"{tag}us", [P, hidden // P])
                    ds = sbuf(sc, f"{tag}ds", [P, D])
                    dso = [sbuf(sc, f"{tag}dso{i}", [P, D]) for i in range(2)]
                    dso = Ring(dso, begin)
                    sp.dma(gs[:], scales[0], begin, mark=S("scales"))
                    sp.dma(us[:], scales[1], mark=S("scales"))
                    sc_in = sp.dma(ds[:], scales[2], mark=S("scales"))

                def load_weights(g, names=(0, 1, 2)):
                    b = g % 2
                    for n in names:
                        src, w_in[b][n] = (gate_d, up_d, down_d)[n], []
                        for i in range(wn // D):
                            cols = slice(i * D, (i + 1) * D)
                            dst = [q[:, cols] for q in w[b][n]]
                            if quantised:
                                job = round_job(src[g][:, cols], dst[0], w_free[b], w_in[b][n],
                                                buffers)
                            else:
                                job = split_job(src[g][:, cols], dst, w_free[b], w_in[b][n])
                            weights.waiting.append(job)

                def gate_up(g, c, n, w_in, h_in):
                    b, wb = n % 2, w[g % 2]
                    views = [[q.rearrange("p (k m) -> p k m", k=KT) for q in wb[i]]
                             for i in range(2)]
                    pairs = ((HI, HI), (HI, LO)) if quantised else THREE
                    done, late = [], None
                    for m in range(MT):
                        mt = g * MT + m
                        ps, ps_free = slots.take(2)
                        toks = []
                        for i in range(2):
                            terms = [(views[i][wp][:, k, m * P:(m + 1) * P], h[c][hp][:, k, :])
                                     for k in range(KT) for wp, hp in pairs]
                            toks.append(passes(ps[:, i, :], terms, ps_free, w_in[g % 2][i], h_in,
                                               mark=S("gate_up")))
                        _, s, s_free = silu.take()
                        _, pr, p_free = prod.take()
                        if quantised:
                            sl = act.do(lambda e, s=s, ps=ps, mt=mt: e.activation(
                                s[:], ps[:, 0, :], ACT.Silu, scale=gs[:, mt:mt + 1]),
                                toks[0], s_free, sc_in, mark=S("silu"))
                            pt = dve.do(lambda e, s=s, ps=ps, pr=pr, mt=mt: e.scalar_tensor_tensor(
                                pr[:], ps[:, 1, :], us[:, mt:mt + 1], s[:], ALU.mult, ALU.mult),
                                toks[1], sl, p_free, sc_in, mark=S("prod"))
                        else:
                            sl = act.do(lambda e, s=s, ps=ps: e.activation(
                                s[:], ps[:, 0, :], ACT.Silu), toks[0], s_free, mark=S("silu"))
                            pt = dve.do(lambda e, s=s, ps=ps, pr=pr: e.tensor_tensor(
                                pr[:], ps[:, 1, :], s[:], ALU.mult), toks[1], sl, p_free,
                                mark=S("prod"))
                        s_free[:] = [pt]
                        ps_free[:] = [sl, pt]
                        hi = act.do(lambda e, pr=pr, m=m: e.activation(
                            act_[b][HI][:, m, :], pr[:], ACT.Copy), pt, a_free[b], mark=S("a_hi"))
                        if late:
                            done.append(late())
                            tick()

                        def late(pr=pr, m=m, hi=hi, p_free=p_free):
                            lo = dve.do(lambda e: e.tensor_tensor(
                                act_[b][LO][:, m, :], pr[:], act_[b][HI][:, m, :].bitcast(F32),
                                ALU.subtract), hi, a_free[b], mark=S("a_lo"))
                            p_free[:] = [lo]
                            return lo
                    done.append(late())
                    tick()
                    h_free[c][:] = [toks[1]]
                    return [done[-1], hi]

                def down(g, c, n, a_in, w_in):
                    b = n % 2
                    wd = [q.rearrange("p (m d) -> p m d", m=MT) for q in w[g % 2][2]]
                    pairs = ((HI, HI), (LO, HI)) if quantised else THREE
                    for i in range(CT):
                        t = c * CT + i
                        if i < 2:
                            _, bank, free = banks.take()
                        else:
                            bank, free = slots.take()
                            bank = bank[:, 0, :]
                        terms = [(act_[b][ap][:, m, i * P:(i + 1) * P], wd[wp][:, m, :])
                                 for m in range(MT) for ap, wp in pairs]
                        y = passes(bank, terms, free, a_in, w_in[g % 2][2], mark=S("down"))
                        if quantised:
                            _, o, o_free = dso.take()
                            ev = dve.do(lambda e, o=o, bank=bank: e.scalar_tensor_tensor(
                                o[:], bank, 0.5, ds[:], ALU.mult, ALU.mult), y, o_free, sc_in,
                                mark=S("x_add"))
                            x_ready[t] = pool.do(lambda e, t=t, o=o: e.tensor_tensor(
                                x[:, t, :], x[:, t, :], o[:], ALU.add), ev, x_ready[t], S_last.get("rstd"),
                                mark=S("x_pool"))
                            o_free[:] = [x_ready[t]]
                            free[:] = [ev]
                        else:
                            x_ready[t] = dve.do(lambda e, t=t, bank=bank: e.scalar_tensor_tensor(
                                x[:, t, :], bank, 0.5, x[:, t, :], ALU.mult, ALU.add), y,
                                x_ready[t], mark=S("x_add"))
                            free[:] = [x_ready[t]]
                        tick()
                    a_free[b][:] = [y]
                    w_free[g % 2][:] = [y]

                w_in = [wmem_in + [None], [None] * 3]
                load_weights(0, (2,))
                h_in = [hA_in[0], hA_in[1], [], []]
                normed = dict(enumerate(hA_jobs))
                pending = None
                n = 0
                for g in range(groups):
                    for c in range(NC):
                        if g == 0 and c < 2:
                            jobs = norm_jobs(c + 2, h[c + 2], h_free[c + 2], h_in[c + 2])
                            norms.waiting += jobs
                            normed[c + 2] = jobs[-1]
                        if g == 0:
                            norms.finish(normed[c])
                        if c == 1 or c == 0 and g > 0:
                            weights.flush()
                        weights.every = 2 if c > 0 else 1
                        if c == 1 and g + 1 < groups:
                            load_weights(g + 1)
                        if g == groups - 1 and then:
                            if c == 1:
                                weights.waiting += then(w_free[0], buffers)
                            if c > 1:
                                hA_norm(c - 2, c - 2)
                        a_in = gate_up(g, c, n, w_in, h_in[c])
                        if pending:
                            down(*pending, w_in)
                        pending = (g, c, n, a_in)
                        n += 1
                down(*pending, w_in)
                weights.every = 1
                weights.flush()
                norms.flush()

        def attention(tag, wd, kv_heads, scale, bias, then, then_fp8):
            grouped = kv_heads < HEADS
            with ExitStack() as sc:
                begin = ends()
                w_free = [[], []]
                buffers = fp8_buffers(sc, tag, 1) if then_fp8 else None
                v = sbuf(sc, f"{tag}v", [P, ST, kv_heads, VW], BF16)
                k_st = sbuf(sc, f"{tag}kst", [P, HPG, SEQ], F32R)
                q_st = sbuf(sc, f"{tag}qst", [P, HPG, SEQ], F32R)
                k_free = [list(begin) for _ in range(HPG)]
                q_free = [list(begin) for _ in range(HPG)]
                stage = {n: [sbuf(sc, f"{tag}{n}s{p}", [P, SEQ], F32R) for p in range(2)]
                         for n in "qk"}
                stage_free = {n: list(begin) for n in "qk"}
                y = sbuf(sc, f"{tag}y", [P, ST, D])
                den = sbuf(sc, f"{tag}den", [P, ST, HEADS])
                y_free = list(begin)
                negmax = Ring([sbuf(sc, f"{tag}negmax{i}", [P, ST]) for i in range(2)], begin)
                mrow = Ring([[sbuf(sc, f"{tag}mrow{i}{p}", [ST, P], F32R) for p in range(2)]
                             for i in range(2)], begin)
                const_in = []
                if bias:
                    rope_d, bq_d, bk_d, bv_d, bo_d = bias
                    rope = {n: sbuf(sc, f"{tag}rope{n}", [P, SEQ]) for n in "qk"}
                    bcol = sbuf(sc, f"{tag}bcol", [P, 4 + 1 + 1])
                    bo = sbuf(sc, f"{tag}bo", [P, D])
                    sp.dma(rope["q"][:], rope_d[0], begin, mark=S("bias"))
                    sp.dma(rope["k"][:], rope_d[1], mark=S("bias"))
                    sp.dma(bcol[:, 0:4], bq_d, mark=S("bias"))
                    sp.dma(bcol[:, 4:5], bk_d, mark=S("bias"))
                    sp.dma(bcol[:, 5:6], bv_d, mark=S("bias"))
                    const_in = [sp.dma(bo[:], bo_d, mark=S("bias"))]

                ones = pool.do(lambda e: e.memset(v[:, :, :, 0:1], 1.0), begin, mark=S("ones"))
                kones = [ones]

                def clear_job(j):
                    clear_q = dve.do(lambda e: e.memset(q_st[3 * HD:P, j, :].bitcast(F32), 0.0),
                                     begin, mark=S("q_clear"))
                    clear_k = pool.do(lambda e: e.memset(k_st[3 * HD:P, j, :].bitcast(F32), 0.0),
                                      begin, kones, pool.last, mark=S("k_ones"))
                    put = pool.do(lambda e: e.memset(
                        k_st[3 * HD:3 * HD + 2, j, :].bitcast(F32), 1.0), clear_k,
                        mark=S("k_ones"))
                    kones[:] = [clear_q, put]
                    pool.need(put)
                    yield

                o_w = [[stage["qk"[k // 2]][p][:, k % 2 * D:(k % 2 + 1) * D] for k in range(KT)]
                       for p in range(2)]

                def v_jobs(free, toks):
                    return [split_job(piece, [q[:, k, :] for q in v_w], free, toks)
                            for k, piece in enumerate(wd["v"])]

                def v_weights(scope, n):
                    return [sbuf(scope, f"{tag}vw{n}{p}", [P, len(wd["v"]), D], F32R)
                            for p in range(2)]

                def piece_job(n, g, i):
                    at, w_in = (0, w_g[g][0]) if n == "q" else (2, w_g[g][1])
                    cols = slice(i * CH // 2, (i + 1) * CH // 2)
                    ps, ps_free = slots.take()
                    src = ps[:, 0, 0:CH // 2]
                    wv = [wmem[:, g % 2, at + p, :].rearrange("p (k m) -> p k m", k=KT)
                          for p in range(2)]
                    terms = [(wv[wp][:, k, :], hA[hp][:, k, cols]) for k in range(KT)
                             for wp, hp in THREE]
                    t = passes(src, terms, ps_free, w_in, hA_in[i // 2], mark=S("proj"))
                    w_free[g % 2][:] = [t]
                    hA_free[i // 2][:] = [t]
                    dst = [q[:, cols] for q in stage[n]]
                    yield
                    if not bias:
                        staged[n] += split_psum(src, dst, t, stage_free[n], ps_free, "qk",
                                                scale=scale if n == "q" else None)
                        return
                    _, buf, free = tmps.take()
                    col = bcol[:, g:g + 1] if n == "q" else bcol[:, 4:5]
                    r = dve.do(lambda e: e.scalar_tensor_tensor(
                        buf[:, 0:CH // 2], src, col, rope[n][:, cols], ALU.add, ALU.mult), t, free,
                        const_in, mark=S("rope"))
                    ps_free[:] = [r]
                    hi = act.do(lambda e: e.activation(dst[HI], buf[:, 0:CH // 2], ACT.Copy), r,
                                stage_free[n], mark=S("qk_hi"))
                    lo = dve.do(lambda e: e.tensor_tensor(dst[LO], buf[:, 0:CH // 2],
                                                          dst[HI].bitcast(F32), ALU.subtract),
                                hi, stage_free[n], mark=S("qk_lo"))
                    free[:] = [lo]
                    staged[n] += [hi, lo]

                def group_jobs(g):
                    names = "qk" if g == 0 or not grouped else "q"
                    for n in names:
                        staged[n] = []
                    return [piece_job(n, g, i) for n in names for i in range(4)]

                def group_weights(g):
                    w_g[g] = [[], []]
                    names = "qk" if g == 0 or not grouped else "q"
                    return [split_job(wd[n][g], [wmem[:, g % 2, 2 * i + p, :] for p in range(2)],
                                      w_free[g % 2], w_g[g][i]) for i, n in enumerate(names)]

                def stack(n, j, ready):
                    st, free = (q_st, q_free) if n == "q" else (k_st, k_free)
                    order = (HI, LO, HI) if n == "q" else (HI, HI, LO)
                    for r, part in enumerate(order):
                        t = sp.dma(st[r * HD:(r + 1) * HD, j, :].bitcast(F32),
                                   stage[n][part][j * HD:(j + 1) * HD, :].bitcast(F32),
                                   ready, free[j], kones, mark=S(f"{n}_st{j}"))
                    if n == "q":
                        t = sp.dma(st[3 * HD:3 * HD + 2, j, :].bitcast(F32), 
                                   k_st[P - 2:P, j, :].bitcast(F32), free[j],
                                   mark=S(f"{n}_st{j}"))
                    return t

                def v_split(tiles, src, ready, src_free):
                    tdims = dict(h=kv_heads, d=HD)
                    parts = [v[:, tiles, :, 1 + i * HD:1 + (i + 1) * HD] for i in range(3)]
                    s = src.rearrange("p (t h d) -> p t h d", **tdims)
                    v1 = act.do(lambda e: e.activation(parts[0], s, ACT.Copy), ready, v_free,
                                mark=S("v1"))
                    _, buf, free = tmps.take()
                    r = buf[:].rearrange("p (t h d) -> p t h d", **tdims)
                    r1 = dve.do(lambda e: e.tensor_tensor(r, s, parts[0], ALU.subtract), v1, free,
                                mark=S("v_rest"))
                    src_free[:] = [r1]
                    yield
                    v2 = act.do(lambda e: e.activation(parts[1], r, ACT.Copy), r1, v_free,
                                mark=S("v2"))
                    v3 = dve.do(lambda e: e.tensor_tensor(parts[2], r, parts[1], ALU.subtract), v2,
                                v_free, mark=S("v3"))
                    free[:] = [v3]
                    v_in.extend([v1, v2, v3])

                def v_tile_job(t):
                    ps, ps_free = slots.take()
                    terms = [(hA[hp][:, k, t * P:(t + 1) * P], v_w[wp][:, k, :])
                             for k in range(KT) for wp, hp in THREE]
                    tok = passes(ps[:, 0, :], terms, ps_free, v_w_in, hA_in[t // CT],
                                 mark=S("v_mm"))
                    hA_free[t // CT][:] = [tok]
                    v_last[0] = tok
                    yield from v_split(slice(t, t + 1), ps[:, 0, :], tok, ps_free)

                def v_chunk_job(c):
                    ps, ps_free = slots.take()
                    wv = [q[:, 0, :].rearrange("p (k m) -> p k m", k=KT) for q in v_w]
                    terms = [(wv[wp][:, k, :], hA[hp][:, k, c * CH:(c + 1) * CH])
                             for k in range(KT) for wp, hp in THREE]
                    t = passes(ps[:, 0, :], terms, ps_free, v_w_in, hA_in[c], mark=S("v_mm"))
                    v_last[0] = t
                    _, buf, free = tmps.take()
                    vb = act.do(lambda e: e.activation(buf[:], ps[:, 0, :], ACT.Identity,
                                                       bias=bcol[:, 5:6]), t, free, const_in,
                                mark=S("v_bias"))
                    ps_free[:] = [vb]
                    yield
                    ps2, ps2_free = slots.take()
                    pe.need(vb, ps2_free)
                    for i in range(CT):
                        tp = pe.do(lambda e, i=i: e.transpose(
                            ps2[:, 0, i * P:(i + 1) * P], buf[:, i * P:(i + 1) * P], ident[:]),
                            mark=S("v_tp"))
                    free[:] = [tp]
                    yield
                    yield from v_split(slice(c * CT, (c + 1) * CT), ps2[:, 0, :], tp, ps2_free)

                norms.flush()
                v_free = []
                v_last = [None]
                w_g = {g: [wmem_in[g][0], wmem_in[g][1]] for g in range(2)}
                e_jobs = Jobs()
                v_w_in = []
                v_scope = sc.enter_context(ExitStack())
                v_w = v_weights(v_scope, 0)
                e_jobs.waiting += v_jobs(begin, v_w_in)
                for b in range(BATCH):
                    staged, v_in = {}, []
                    first, clears = Jobs(), Jobs()
                    if b == 0:
                        clears.waiting += [clear_job(j) for j in range(HPG)]
                    first.waiting += group_jobs(0)
                    while first.waiting or first.running:
                        first.tick()
                        e_jobs.tick()
                        clears.tick()
                    e_jobs.flush()
                    clears.flush()
                    q_in = [None] * HPG
                    if not grouped or b == 0:
                        k_in = [None] * HPG

                    def stack_head(n, j):
                        token = stack(n, j, list(staged[n]))
                        (q_in if n == "q" else k_in)[j] = token
                        stage_free[n][:] = stage_free[n][-(HPG - 1):] + [token]

                    for j in range(HPG):
                        for n in "qk":
                            stack_head(n, j)

                    def halves(ps, width):
                        return ps[:, 0:1, 0:width] if width <= CH else ps[:, :, 0:width // 2]

                    def head_of(n):
                        g, j = n // HPG, n % HPG
                        return (HPG * j + g, j, j) if grouped else (n, j, n)

                    def row_max(n, i, out_, out_free):
                        _, j, _ = head_of(n)
                        w_ = (i + 1) * P
                        cols = max(w_, 2 * P)
                        pieces = 1 if cols <= CH else 2
                        ps, ps_free = slots.take(pieces)
                        pe.need(ps_free, q_in[j], k_in[j], consts)
                        pw = cols // pieces
                        for z in range(pieces):
                            pe.do(mm(ps[:, z, 0:pw], q_st[:, j, i * P:(i + 1) * P],
                                     k_st[:, j, z * pw:(z + 1) * pw], True, True))
                        end = w_ - (pieces - 1) * pw
                        t = pe.do(mm(ps[:, pieces - 1, end - P:end], ident_b[:], mask_q[:], False,
                                     True, True), mark=S("s_q"))
                        mx = dve.do(lambda e: e.tensor_reduce(
                            out_[:, i:i + 1], halves(ps, w_), AX.XY, ALU.max, negate=True), t,
                            out_free, mark=S("row_max"))
                        ps_free[:] = [mx]
                        return mx

                    def max_job(n, mx, nm, nm_free):
                        _, j, _ = head_of(n)
                        yield
                        ps, ps_free = slots.take()
                        tp = pe.do(lambda e: e.transpose(ps[0:ST, 0, 0:P], nm[:], ident[:]),
                                   mx, ps_free, mark=S("m_tp"))
                        nm_free[:] = [tp]
                        _, mr, mr_free = mrow.take()
                        hi = act.do(lambda e: e.activation(mr[HI][:], ps[0:ST, 0, 0:P], ACT.Copy),
                                    tp, mr_free, mark=S("m_row"))
                        yield
                        lo = dve.do(lambda e: e.tensor_tensor(mr[LO][:], ps[0:ST, 0, 0:P],
                                                              mr[HI][:].bitcast(F32),
                                                              ALU.subtract), hi, mark=S("m_low"))
                        ps_free[:] = [lo]
                        for p, ready in enumerate((hi, lo)):
                            row = q_st[3 * HD + p:3 * HD + p + 1, j, :].bitcast(F32)
                            t = sp.dma(row.rearrange("o (i q) -> o i q", q=P),
                                       mr[p][:].bitcast(F32), ready, q_free[j],
                                       mark=S(f"m_in{n % 2}"))
                        mr_free[:] = [t]
                        m_in[n] = t

                    def exp_keys(n, jt, m_in):
                        head, j, kv = head_of(n)
                        w_ = SEQ - jt * P
                        cols = max(w_, 2 * P)
                        pieces = 1 if cols <= CH else 2
                        pw, q0 = cols // pieces, SEQ - cols
                        skip = cols - w_
                        (e_,), e_free = e32.take(w_)
                        w_in, ex = [m_in, kones], []
                        for z in range(pieces):
                            ps, ps_free = slots.take()
                            ps = ps[:, 0, 0:pw]
                            t = pe.do(mm(ps, k_st[:, j, jt * P:(jt + 1) * P],
                                         q_st[:, j, q0 + z * pw:q0 + (z + 1) * pw],
                                         True, True), ps_free, w_in,
                                      mark=S("s_k") if z > 0 else None)
                            if z == 0:
                                t = pe.do(mm(ps[:, skip:skip + P], ident_b[:], mask_k[:], False,
                                             True, True), mark=S("s_k"))
                            src, at = ps[:, skip:pw], slice(z * pw, (z + 1) * pw - skip)
                            ex.append(act.do(lambda e, src=src, at=at: e.activation(
                                e_[:, at], src, ACT.Exp, bias=p_scale[:]), t, e_free, consts,
                                mark=S("exp")))
                            ps_free[:] = [ex[-1]]
                        if jt == ST - 1:
                            q_free[j][:] = [t]
                            if not grouped or n // HPG == HPG - 1:
                                k_free[j][:] = [t]
                        return n, jt, w_, e_, e_free, ex

                    def split_exp(n, jt, w_, e_, e_free, ex):
                        (eh, el), e16_free = e16.take(w_)
                        if jt in HI_ON_ACT:
                            hi = act.do(lambda e: e.activation(eh, e_, ACT.Copy), ex, e16_free,
                                        mark=S("p_hi_act"))
                        else:
                            hi = dve.do(lambda e: e.tensor_copy(eh, e_), ex, e16_free,
                                        mark=S("p_hi_dve"))
                        cut, los = LO_ON_POOL[jt] * P, []
                        for lane, nm, cols in ((pool, "p_lo_pool", slice(0, cut)),
                                               (dve, "p_lo_dve", slice(cut, w_))):
                            if cols.start < cols.stop:
                                los.append(lane.do(lambda e, cols=cols: e.tensor_tensor(
                                    el[:, cols], e_[:, cols], eh[:, cols], ALU.subtract), hi,
                                    e16_free, mark=S(nm)))
                        e_free[:] = los
                        return n, jt, eh, el, [hi, los], e16_free

                    acc_free = banks.free

                    def times_v(n, jt, eh, el, ready, e16_free):
                        head, _, kv = head_of(n)
                        pe.need(ready, v_in, ones)
                        if jt == 0:
                            pe.need(acc_free[0], acc_free[1])
                        for i in range(jt, ST):
                            o = acc[:, i // CT, i % CT * VW:i % CT * VW + 1 + 3 * HD]
                            q = slice((i - jt) * P, (i - jt + 1) * P)
                            first = jt == 0 and i % CT == 0
                            pe.do(mm(o, eh[:, q], v[:, jt, kv, 0:1 + 3 * HD], first, False, True))
                            t = pe.do(mm(o[:, 0:1 + 2 * HD], el[:, q], v[:, jt, kv, 0:1 + 2 * HD],
                                         False, i == jt, True),
                                      mark=S("pv") if i in (CT - 1, ST - 1) or i == jt else None)
                            if i == jt and i in (CT - 1, ST - 1):
                                take_y(n, i // CT, t)
                        e16_free[:] = [t]

                    def take_y(n, bank, t):
                        head, _, _ = head_of(n)
                        o = acc[:, bank, 0:CT * VW].rearrange("p (i w) -> p i w", w=VW)
                        parts = o[:, :, 1:1 + 3 * HD].rearrange("p i (s d) -> p i d s", s=3)
                        i0 = bank * CT
                        dve.do(lambda e: e.tensor_reduce(
                            y[:, i0:i0 + CT, head * HD:(head + 1) * HD], parts, AX.X, ALU.add), t,
                            y_free, mark=S("y_take"))
                        r = dve.do(lambda e: e.tensor_copy(den[:, i0:i0 + CT, head:head + 1],
                                                           o[:, :, 0:1]), t, y_free,
                                   mark=S("y_take"))
                        acc_free[bank][:] = [r]
                        taken[0] = r

                    taken = [None]
                    m_in = {}
                    nm_out = [None, None]

                    def row_unit(u):
                        n, i = divmod(u, ST)
                        if n < HEADS:
                            if i == 0:
                                _, nm_out[0], nm_out[1] = negmax.take()
                            mx = row_max(n, (u - AHEAD) % ST, *nm_out)
                            if i == ST - 1:
                                side.start(max_job(n, mx, *nm_out))

                    if bias:
                        for t in range(b * ST, (b + 1) * ST):
                            x_ready[t] = pool.do(lambda e, t=t: e.tensor_tensor(
                                x[:, t, :], x[:, t, :], bo[:], ALU.add), S_last["rstd"],
                                x_ready[t], const_in, mark=S("x_pool"))
                    side = Jobs()
                    if grouped:
                        side.waiting += [v_chunk_job(c) for c in range(2)]
                    else:
                        side.waiting += [v_tile_job(t) for t in range(ST)]
                    tiles, wait = len(side.waiting), 2
                    for u in range(-wait, AHEAD):
                        side.tick(start=(u + wait) * tiles // (AHEAD + wait)
                                  != (u + wait - 1) * tiles // (AHEAD + wait))
                        if u >= 0:
                            row_unit(u)
                    side.flush()
                    v_scope.close()
                    heads_scope = sc.enter_context(ExitStack())
                    e32 = Strip([sbuf(heads_scope, f"{tag}e32{b}", [P, E32])], [v_last[0]])
                    e16 = Strip([sbuf(heads_scope, f"{tag}e16{b}{p}", [P, 4 * SEQ], F16)
                                 for p in range(2)], [v_last[0]])

                    GU = HPG * ST
                    beside = {}
                    o_in = []
                    last = (HPG - 1) * GU
                    fresh, behind = [], []
                    for u in range(HEADS * ST):
                        n, i = divmod(u, ST)
                        g, at = divmod(u, GU)
                        if at == 0 and g + 1 < HPG:
                            beside.update({u + 2 * k: job for k, job in
                                           enumerate(group_jobs(g + 1))})
                        if at == 20 and g + 2 < HPG:
                            beside.update({u + 2 * k: job for k, job in
                                           enumerate(group_weights(g + 2))})
                        if u == last + 2:
                            jobs = [split_job(wd["o"][k], [o_w[p][k] for p in range(2)],
                                              [stage_free["q"], stage_free["k"]], o_in)
                                    for k in range(KT)]
                            w_all = [w_free[0][:], w_free[1][:]]
                            if b + 1 < BATCH:
                                jobs += group_weights(0) + group_weights(1)
                            elif then:
                                jobs += then(w_all, buffers)
                            step = (GU - 4) // len(jobs)
                            beside.update({u + step * k: job for k, job in enumerate(jobs)})
                        side.tick(start=False)
                        row_unit(u + AHEAD)
                        fresh.append(exp_keys(n, i, m_in[n]))
                        if len(fresh) > SPLIT_LAG:
                            behind.append(split_exp(*fresh.pop(0)))
                        if len(behind) > PV_LAG:
                            times_v(*behind.pop(0))
                        if u in beside:
                            side.start(beside.pop(u))
                        if g + 1 < HPG:
                            for j, when in enumerate((17, 18, 24, 31)):
                                if at == when:
                                    for m in "qk" if not grouped else "q":
                                        stack_head(m, j)
                    side.flush()
                    behind += [split_exp(*unit) for unit in fresh]
                    for unit in behind:
                        times_v(*unit)
                    v_free[:] = [pe.last]

                    now = ends()
                    heads_scope.close()
                    if b + 1 < BATCH:
                        v_w_in = []
                        v_scope = sc.enter_context(ExitStack())
                        v_w = v_weights(v_scope, b + 1)
                        e_jobs.waiting += v_jobs(now, v_w_in)
                    proj_scope = sc.enter_context(ExitStack())
                    yT = Ring([[sbuf(proj_scope, f"{tag}yT{b}{i}{p}", [P, KT, P], F32R)
                                for p in range(2)] for i in range(2)], now)
                    if b + 1 < BATCH or then:
                        for half in range(2):
                            hA_norm(half + 2 if b + 1 < BATCH else half, half)
                    rec = dve.do(lambda e: e.reciprocal(den[:], den[:]), taken[0], mark=S("recip"))

                    normalised = []
                    for t in range(ST):
                        lane, nm = (dve, "y_norm_dve") if t in (0, 2) else (pool, "y_norm")
                        normalised.append(lane.do(lambda e, t=t: e.tensor_tensor(
                            y[:, t, :].rearrange("p (h d) -> p h d", d=HD),
                            y[:, t, :].rearrange("p (h d) -> p h d", d=HD),
                            den[:, t, :].unsqueeze(2).to_broadcast([P, HEADS, HD]), ALU.mult), rec,
                            mark=S(nm)))

                    def turn(t):
                        yn = normalised[t]
                        ps, ps_free = slots.take()
                        pe.need(yn, ps_free)
                        for k in range(KT):
                            tp = pe.do(lambda e, k=k: e.transpose(
                                ps[:, 0, k * P:(k + 1) * P], y[:, t, k * P:(k + 1) * P], ident[:]),
                                mark=S("y_tp") if k == KT - 1 else None)
                        src = ps[:, 0, :].rearrange("p (k q) -> p k q", k=KT)
                        _, yt, yT_free = yT.take()
                        toks = split_psum(src, [q[:] for q in yt], tp, yT_free, ps_free, "y")
                        y_free[:] = [tp]
                        return yt, toks, yT_free

                    def project_out(t, yt, toks, yT_free):
                        i, bank, free = banks.take()
                        terms = [(yt[yp][:, k, :], o_w[wp][k]) for k in range(KT)
                                 for wp, yp in THREE]
                        o = passes(bank, terms, free, toks, o_in, mark=S("o_proj"))
                        yT_free[:] = [o]
                        tt = b * ST + t
                        x_ready[tt] = dve.do(lambda e: e.tensor_tensor(
                            x[:, tt, :], bank, x[:, tt, :], ALU.add), o, x_ready[tt],
                            S_last["rstd"], mark=S("x_add"))
                        free[:] = [x_ready[tt]]
                        for n in "qk":
                            stage_free[n][:] = [o]

                    turned = turn(0)
                    for t in range(ST):
                        now_, turned = turned, turn(t + 1) if t + 1 < ST else None
                        norms.tick()
                        e_jobs.tick()
                        project_out(t, *now_)
                    norms.flush()
                    proj_scope.close()

        AHEAD = 12
        E32 = 2816
        SPLIT_LAG = 1
        PV_LAG = 2
        HI_ON_ACT = (2, 5)
        LO_ON_POOL = (8, 7, 6, 0, 4, 3, 2, 0)

        ffn0 = ("f0", a["gate0"], a["up0"], a["down0"], 1536, 384,
                (a["gscale"], a["uscale"], a["dscale"].partition_broadcast(P)), True)
        ffn1 = ("f1", a["gate1"], a["up1"], a["down1"], 2048, 256, None, False)
        score_scale = float(1.0 / np.sqrt(np.float32(HD)))
        w0 = {n: [a[n + "0"][i] for i in range(k)] for n, k in
              (("q", 4), ("k", 1), ("v", 1), ("o", 4))}
        w1 = {n: [a[n + "1"][i] for i in range(4)] for n in "qkvo"}
        def first_weights(stage):
            if stage == "f0":
                return (lambda free, buffers: ffn_first_weights(*ffn0[1:3], True, free, buffers)), True
            if stage == "f1":
                return (lambda free, buffers: ffn_first_weights(*ffn1[1:3], False, free, None)), False
            return (lambda free, buffers: attention_first_weights(
                w0 if stage == "a0" else w1, free)), False

        def attention_first_weights(wd, free):
            toks, jobs = [[[], []], [[], []]], []
            for g in range(2):
                for i, n in enumerate("qk"):
                    if g < len(wd[n]):
                        jobs.append(split_job(wd[n][g], [wmem[:, g, 2 * i + p, :]
                                                         for p in range(2)], free, toks[g][i]))
            wmem_in[:] = toks
            return jobs

        with ExitStack() as sc:
            load, fp8 = first_weights(STAGES[0])
            hA_norm(0, 0)
            weights.waiting += load([], fp8_buffers(sc, "first", 3) if fp8 else None)
            tick()
            x_ready += [sp.dma(x[:, t, :], x_rows[t], mark=S(f"x_in{t}"))
                        for t in range(CT, 2 * CT)]
            tick()
            x_ready += [sp.dma(x[:, t, :], x_rows[t], mark=S(f"x_in{t}"))
                        for t in range(2 * CT, NT)]
            while weights.waiting or weights.running or norms.waiting or norms.running:
                tick()
            hA_norm(1, 1)

        for n, s in enumerate(STAGES):
            then, fp8 = first_weights(STAGES[n + 1]) if n + 1 < len(STAGES) else (None, False)
            if s == "f0":
                ffn(f"s{n}" + ffn0[0], *ffn0[1:], then)
            elif s == "f1":
                ffn(f"s{n}" + ffn1[0], *ffn1[1:], then)
            elif s == "a0":
                attention("a0", w0, KV0, score_scale,
                          (a["rope"], a["bq"], a["bk"], a["bv"], a["bo"].partition_broadcast(P)),
                          then, fp8)
            else:
                attention("a1", w1, HEADS, score_scale, None, then, fp8)

        out_rows = out.rearrange("(t p) d -> t p d", p=P)
        for t in range(NT):
            done = sp.dma(out_rows[t], x[:, t, :], x_ready[t], mark=S("out"))
        sp.need(done)

        with nc.Block() as block:
            block.sync(sp.play)
            block.tensor(pe.play)
            block.scalar(act.play)
            block.vector(dve.play)
            block.gpsimd(pool.play)


STAGES = ("f0", "a0", "f0", "f1", "a1", "f1")


def rope_table():
    inv = np.float32(10000.0) ** (np.float32(-2.0) * np.arange(HD // 2, dtype=np.float32)
                                  / np.float32(HD))
    theta = np.arange(SEQ, dtype=np.float32)[:, None] * inv[None, :]
    table = np.tile((np.cos(theta) + np.sin(theta)).T, (2 * HPG, 1)).astype(np.float32)
    return np.stack([table / np.sqrt(np.float32(HD)), table]).astype(np.float32)


def layouts(i):
    def gate(w, gw):
        n = w.shape[1] // gw
        return w.reshape(KT, P, n, gw).transpose(2, 1, 0, 3).reshape(n, P, KT * gw)

    def down(w, gw):
        n = w.shape[0] // gw
        return w.reshape(n, gw // P, P, D).transpose(0, 2, 1, 3).reshape(n, P, gw // P * D)

    def cols(w):
        n = w.shape[1] // P
        return w.reshape(KT, P, n, P).transpose(2, 1, 0, 3).reshape(n, P, KT * P)

    def rows(w):
        return w.reshape(KT, P, D)

    def regroup(w):
        return w.reshape(*w.shape[:-1], HPG, HPG, HD).swapaxes(-3, -2).reshape(w.shape)

    wa = i["L1_attn_w_attn"]
    return {
        "x": i["L0_attn_x"].reshape(TOK, D),
        "gate0": gate(i["L0_ffn_gate_w"], 384), "up0": gate(i["L0_ffn_up_w"], 384),
        "down0": down(i["L0_ffn_down_w"], 384),
        "gscale": i["L0_ffn_gate_scale"].reshape(-1, P).T,
        "uscale": i["L0_ffn_up_scale"].reshape(-1, P).T,
        "dscale": i["L0_ffn_down_scale"],
        "gate1": gate(i["L1_ffn_w_gate"].T, 256), "up1": gate(i["L1_ffn_w_up"].T, 256),
        "down1": down(i["L1_ffn_w_down"].T, 256),
        "q0": cols(regroup(i["L0_attn_Wq"].T)), "k0": cols(i["L0_attn_Wk"].T),
        "v0": cols(i["L0_attn_Wv"].T), "o0": rows(i["L0_attn_Wo"].T),
        "bq": regroup(i["L0_attn_bq"]).reshape(HPG, P).T, "bk": i["L0_attn_bk"].reshape(P, 1),
        "bv": i["L0_attn_bv"].reshape(P, 1), "bo": i["L0_attn_bo"],
        "q1": cols(wa[:, 0:D]), "k1": cols(wa[:, D:2 * D]), "v1": rows(wa[:, 2 * D:3 * D]),
        "o1": rows(i["L1_attn_w_proj"]),
        "rope": rope_table(),
    }


def kernel(**inputs):
    import concourse.bacc as bacc
    from concourse.bass_utils import run_bass_kernel_spmd

    arrays = {f"in_{n}": np.ascontiguousarray(v) for n, v in
              layouts({n: np.asarray(v) for n, v in inputs.items()}).items()}
    nc = bacc.Bacc("TRN2", target_bir_lowering=False, num_devices=1)
    aps = {n[3:]: nc.dram_tensor(n, v.shape, F32, kind="ExternalInput").ap() for n, v in arrays.items()}
    out = nc.dram_tensor("out", (TOK, D), F32, kind="ExternalOutput").ap()
    build(nc, aps, out)
    r = run_bass_kernel_spmd(nc, [arrays], core_ids=[0])
    return r.results[0]["out"].reshape(BATCH, SEQ, D)
```
